# Optimizing a Trainium2 kernel written in Bass

```python
import numpy as np
import jax
import jax.numpy as jnp

def _softmax(x, axis=-1):
    return jax.nn.softmax(x, axis=axis)

def _gelu(x):
    return jax.nn.gelu(x, approximate=True)

def _silu(x):
    return jax.nn.silu(x)

def _sigmoid(x):
    return jax.nn.sigmoid(x)

def _layernorm(x, axis=-1, eps=1e-05):
    m = jnp.mean(x, axis=axis, keepdims=True)
    v = jnp.var(x, axis=axis, keepdims=True)
    return (x - m) / jnp.sqrt(v + eps)

def _scatter_add(tgt, idx, src, axis=0):
    return tgt.at[idx].add(src)

def _segment_sum(src, seg, n):
    return jax.ops.segment_sum(src, seg, n)
kernel_name = 'mk_vit_tower_postln_d1_tok_img256_r4_d5a28e'

def setup_inputs(seed: int=0):
    np.random.seed(seed)
    _w = jnp.asarray

    def _rec_inputs():
        import jax
        import jax.numpy as jnp
        _rk = jax.random.key(seed)
        x = -7.10856e-05 + 0.999911 * jax.random.normal(jax.random.fold_in(_rk, 1), (64, 1, 256, 256), jnp.float32)
        return x
    x = _rec_inputs()

    def _L0_tok_setup():
        import jax, jax.numpy as jnp
        import numpy as np
        INV_SQRT2 = 0.7071067811865476

        def haar_dwt2(x):
            lo = (x[..., ::2] + x[..., 1::2]) * INV_SQRT2
            hi = (x[..., ::2] - x[..., 1::2]) * INV_SQRT2
            cA = (lo[..., ::2, :] + lo[..., 1::2, :]) * INV_SQRT2
            cH = (lo[..., ::2, :] - lo[..., 1::2, :]) * INV_SQRT2
            cV = (hi[..., ::2, :] + hi[..., 1::2, :]) * INV_SQRT2
            cD = (hi[..., ::2, :] - hi[..., 1::2, :]) * INV_SQRT2
            return (cA, (cH, cV, cD))

        def wavedec2_maps(x, levels):
            a = x
            details = []
            for _ in range(levels):
                a, d = haar_dwt2(a)
                details.append(d)
            maps = [a]
            for d in reversed(details):
                maps.extend(d)
            return maps
        key = jax.random.key(seed)
        k1, k2 = jax.random.split(key)
        B, H, W_img = (64, 256, 256)
        x = jax.random.normal(k1, (B, 1, H, W_img), dtype=jnp.float32)
        n_maps = 1 + 3 * 2
        W = jax.random.normal(k2, (n_maps, 64), dtype=jnp.float32) * (1.0 / np.sqrt(n_maps))
        b = jnp.zeros((64,), dtype=jnp.float32)
        return {'x': x, 'W': W, 'b': b}
    _L0_tok_all = _L0_tok_setup()
    _L0_tok_in = {k: v for k, v in _L0_tok_all.items() if k in ('W', 'b')}
    del _L0_tok_all

    def _L0_attn_setup():
        import jax, jax.numpy as jnp
        import numpy as np
        HEADS = 8
        EPS = 1e-05

        def _ln(t, w, b, headc):
            m = jnp.mean(t, axis=-1, keepdims=True)
            d = t - m
            std = jnp.sqrt(jnp.sum(d * d, axis=-1, keepdims=True) / (headc - 1))
            return w * (d / (std + EPS)) + b
        key = jax.random.key(seed)
        B, N, C = (32, 1024, 64)
        headc = C // HEADS
        x = jax.random.normal(key, (B, N, C), dtype=jnp.float32)
        return {'x': x, 'kln_weight': jnp.ones((HEADS, 1, headc), dtype=jnp.float32), 'kln_bias': jnp.zeros((HEADS, 1, headc), dtype=jnp.float32), 'vln_weight': jnp.ones((HEADS, 1, headc), dtype=jnp.float32), 'vln_bias': jnp.zeros((HEADS, 1, headc), dtype=jnp.float32)}
    _L0_attn_all = _L0_attn_setup()
    _L0_attn_in = {k: v for k, v in _L0_attn_all.items() if k in ('kln_weight', 'kln_bias', 'vln_weight', 'vln_bias')}
    del _L0_attn_all

    def _L0_ffn_setup():
        import jax, jax.numpy as jnp
        import numpy as np
        NUM_EXPERTS = 8
        TOP_K = 2
        B, S, D = (8, 2048, 64)

        def _moe(tokens, router_w, w1, b1, w2, b2):
            N = tokens.shape[0]
            E = router_w.shape[0]
            logits = tokens.astype(jnp.float32) @ router_w.astype(jnp.float32).T
            probs = jax.nn.softmax(logits, axis=-1)
            rw, re = jax.lax.top_k(probs, TOP_K)
            if TOP_K > 1:
                rw = rw / jnp.maximum(rw.sum(-1, keepdims=True), 1e-12)
            rw = rw.astype(tokens.dtype)
            combine = jnp.zeros((N, E), tokens.dtype).at[jnp.arange(N)[:, None], re].set(rw)
            out = tokens
            for e in range(E):
                h = jax.nn.gelu(tokens @ w1[e] + b1[e], approximate=False)
                y = h @ w2[e] + b2[e]
                out = out + combine[:, e:e + 1] * y
            return out
        key = jax.random.key(seed)
        ks = jax.random.split(key, 4)
        scale = 1.0 / np.sqrt(D).astype(np.float32)
        return {'input_embeddings': jax.random.normal(ks[0], (B, S, D), jnp.float32), 'router_w': jax.random.normal(ks[1], (NUM_EXPERTS, D), jnp.float32) * scale, 'w1': jax.random.normal(ks[2], (NUM_EXPERTS, D, D), jnp.float32) * scale, 'b1': jnp.zeros((NUM_EXPERTS, D), jnp.float32), 'w2': jax.random.normal(ks[3], (NUM_EXPERTS, D, D), jnp.float32) * scale, 'b2': jnp.zeros((NUM_EXPERTS, D), jnp.float32)}
    _L0_ffn_all = _L0_ffn_setup()
    _L0_ffn_in = {k: v for k, v in _L0_ffn_all.items() if k in ('router_w', 'w1', 'b1', 'w2', 'b2')}
    del _L0_ffn_all
    return {'x': x, 'L0_tok_W': _L0_tok_in['W'], 'L0_tok_b': _L0_tok_in['b'], 'L0_attn_kln_weight': _L0_attn_in['kln_weight'], 'L0_attn_kln_bias': _L0_attn_in['kln_bias'], 'L0_attn_vln_weight': _L0_attn_in['vln_weight'], 'L0_attn_vln_bias': _L0_attn_in['vln_bias'], 'L0_ffn_router_w': _L0_ffn_in['router_w'], 'L0_ffn_w1': _L0_ffn_in['w1'], 'L0_ffn_b1': _L0_ffn_in['b1'], 'L0_ffn_w2': _L0_ffn_in['w2'], 'L0_ffn_b2': _L0_ffn_in['b2']}

def reference(x, L0_tok_W, L0_tok_b, L0_attn_kln_weight, L0_attn_kln_bias, L0_attn_vln_weight, L0_attn_vln_bias, L0_ffn_router_w, L0_ffn_w1, L0_ffn_b1, L0_ffn_w2, L0_ffn_b2):
    import jax
    import jax.numpy as jnp

    def _L0_tok_ref(x, W, b):
        import jax, jax.numpy as jnp
        import numpy as np
        INV_SQRT2 = 0.7071067811865476

        def haar_dwt2(x):
            lo = (x[..., ::2] + x[..., 1::2]) * INV_SQRT2
            hi = (x[..., ::2] - x[..., 1::2]) * INV_SQRT2
            cA = (lo[..., ::2, :] + lo[..., 1::2, :]) * INV_SQRT2
            cH = (lo[..., ::2, :] - lo[..., 1::2, :]) * INV_SQRT2
            cV = (hi[..., ::2, :] + hi[..., 1::2, :]) * INV_SQRT2
            cD = (hi[..., ::2, :] - hi[..., 1::2, :]) * INV_SQRT2
            return (cA, (cH, cV, cD))

        def wavedec2_maps(x, levels):
            a = x
            details = []
            for _ in range(levels):
                a, d = haar_dwt2(a)
                details.append(d)
            maps = [a]
            for d in reversed(details):
                maps.extend(d)
            return maps
        imgs = x[:, 0]
        B = imgs.shape[0]
        maps = wavedec2_maps(imgs, 2)
        proc = [jax.image.resize(m, (B, 8, 8), method='bilinear') for m in maps]
        feat = jnp.stack(proc, axis=1)
        feat = feat.reshape(B, feat.shape[1], 64).transpose(0, 2, 1)
        return feat @ W + b

    def _L0_attn_ref(x, kln_weight, kln_bias, vln_weight, vln_bias):
        import jax, jax.numpy as jnp
        import numpy as np
        HEADS = 8
        EPS = 1e-05

        def _ln(t, w, b, headc):
            m = jnp.mean(t, axis=-1, keepdims=True)
            d = t - m
            std = jnp.sqrt(jnp.sum(d * d, axis=-1, keepdims=True) / (headc - 1))
            return w * (d / (std + EPS)) + b
        B, N, C = x.shape
        headc = C // HEADS
        qkv = x.reshape(B, N, HEADS, headc).transpose(0, 2, 1, 3)
        k = _ln(qkv, kln_weight, kln_bias, headc)
        v = _ln(qkv, vln_weight, vln_bias, headc)
        kv = jnp.einsum('bhnd,bhne->bhde', k, v) / N
        out = jnp.einsum('bhnd,bhde->bhne', qkv, kv)
        out = out.transpose(0, 2, 1, 3).reshape(B, N, C)
        return out + x

    def _L0_ffn_ref(input_embeddings, router_w, w1, b1, w2, b2):
        import jax, jax.numpy as jnp
        import numpy as np
        NUM_EXPERTS = 8
        TOP_K = 2
        B, S, D = (8, 2048, 64)

        def _moe(tokens, router_w, w1, b1, w2, b2):
            N = tokens.shape[0]
            E = router_w.shape[0]
            logits = tokens.astype(jnp.float32) @ router_w.astype(jnp.float32).T
            probs = jax.nn.softmax(logits, axis=-1)
            rw, re = jax.lax.top_k(probs, TOP_K)
            if TOP_K > 1:
                rw = rw / jnp.maximum(rw.sum(-1, keepdims=True), 1e-12)
            rw = rw.astype(tokens.dtype)
            combine = jnp.zeros((N, E), tokens.dtype).at[jnp.arange(N)[:, None], re].set(rw)
            out = tokens
            for e in range(E):
                h = jax.nn.gelu(tokens @ w1[e] + b1[e], approximate=False)
                y = h @ w2[e] + b2[e]
                out = out + combine[:, e:e + 1] * y
            return out
        b, s, d = input_embeddings.shape
        tokens = input_embeddings.reshape(b * s, d)
        return _moe(tokens, router_w, w1, b1, w2, b2).reshape(b, s, d)
    h = _L0_tok_ref(x, L0_tok_W, L0_tok_b)
    h = _layernorm(h + _L0_attn_ref(h, L0_attn_kln_weight, L0_attn_kln_bias, L0_attn_vln_weight, L0_attn_vln_bias), axis=-1)
    h = _layernorm(h + _L0_ffn_ref(h, L0_ffn_router_w, L0_ffn_w1, L0_ffn_b1, L0_ffn_w2, L0_ffn_b2), axis=-1)
    return h

_drawn_inputs = setup_inputs


def setup_inputs(seed=0):
    import zlib

    import numpy as np

    out = dict(_drawn_inputs(seed))
    spreads = {'L0_tok_b': (0.0, 0.1),
     'L0_attn_kln_weight': (1.0, 0.2),
     'L0_attn_kln_bias': (0.0, 0.1),
     'L0_attn_vln_weight': (1.0, 0.2),
     'L0_attn_vln_bias': (0.0, 0.1),
     'L0_ffn_b1': (0.0, 0.326),
     'L0_ffn_b2': (0.0, 0.1)}
    factors = {}
    for name, (base, spread) in spreads.items():
        noise = np.random.default_rng([zlib.crc32(name.encode()), seed]).standard_normal(out[name].shape)
        drawn = base * np.exp(spread * noise) if base else spread * noise
        out[name] = jnp.asarray(drawn.astype(out[name].dtype))
    for name, factor in factors.items():
        out[name] = (out[name] * factor).astype(out[name].dtype)
    return out
```

```python
from contextlib import ExitStack

import numpy as np

import concourse.bass as bass
from concourse import mybir

IMAGES, SIDE = 64, 256
GRID = 8
TOKENS = GRID * GRID
C = 64
HEADS = 8
HEAD = C // HEADS
EXPERTS = 8
FF = 64
KINDS = 4
OPS = KINDS * GRID

CHUNK = 8
CHUNKS = IMAGES // CHUNK
TILES = CHUNK * TOKENS // 128
CT = CHUNK * TOKENS
GROUPS = CHUNK // 2
PAIRS = EXPERTS // 2
SPLIT = 3

LOW1, HIGH1, LOW2, HIGH2 = range(KINDS)
MAPS = [(LOW2, LOW2), (HIGH2, LOW2), (LOW2, HIGH2), (HIGH2, HIGH2),
        (HIGH1, LOW1), (LOW1, HIGH1), (HIGH1, HIGH1)]

_FIELDS = [("rows_op", 2 * OPS), ("cols_op", 2 * OPS), ("ident", 128), ("jmask", GRID),
           ("headmask", C), ("twice", C), ("wtok", C), ("btok", C), ("btok_col", 1),
           ("kw", C), ("kb", C), ("vw", C), ("vb", C), ("w1", 2 * 2 * FF), ("b1", PAIRS),
           ("w2", PAIRS * C), ("router", EXPERTS), ("b2", C), ("select", PAIRS * 128),
           ("before", EXPERTS * EXPERTS), ("rank_limit", TILES * EXPERTS)]
AT, _at = {}, 0
for _name, _n in _FIELDS:
    AT[_name] = (_at, _at + _n)
    _at += _n
PARAMS = _at


def vit_tower_kernel(nc, x, params, out):
    fp32, bf16 = mybir.dt.float32, mybir.dt.bfloat16
    ALU, ACT, AX = mybir.AluOpType, mybir.ActivationFunctionType, mybir.AxisListType

    x_v = x.rearrange("(c n) one (p s) w -> c p n (one s w)", n=CHUNK, s=2)
    out_v = out.rearrange("(c t two) k w -> c (two k) t w", t=TILES, two=2)

    with ExitStack() as ctx:
        def sb(name, shape, dt=fp32):
            return ctx.enter_context(nc.sbuf_tensor(name, shape, dt))

        def ps(name):
            return ctx.enter_context(nc.psum_tensor(name, [128, 512], fp32))

        def sem(name):
            return ctx.enter_context(nc.semaphore(name))

        par_sb = sb("par_sb", [128, PARAMS])

        def P(name):
            return par_sb[:, AT[name][0]:AT[name][1]]

        xt = [sb(f"xt{i}", [128, CHUNK, 2, SIDE]) for i in range(2)]
        rows = sb("rows", [128, 512])
        cols = sb("cols", [128, 2, 2, GROUPS, KINDS, GRID])
        expand = sb("expand", [128, CHUNK, GRID, GRID])
        h_t = sb("h_t", [128, TILES, TOKENS])
        d = sb("d", [128, TILES, C])
        dsq = sb("dsq", [128, TILES, C])
        dss = sb("dss", [128, TILES * HEADS])
        dvar = sb("dvar", [128, TILES * HEADS])
        dstd = sb("dstd", [128, TILES * HEADS])
        dste = sb("dste", [128, TILES * HEADS])
        drec = sb("drec", [128, TILES * HEADS])
        n = sb("n", [128, TILES, C])
        k0 = sb("k0", [128, TILES, C])
        v0 = sb("v0", [128, TILES, C])
        k = sb("k", [128, TILES, C])
        v = sb("v", [128, TILES, C])
        gm = sb("gm", [128, TILES, C])
        kv = sb("kv", [128, TILES, C])
        ysum = sb("ysum", [128, TILES])
        yc = sb("yc", [128, TILES, C])
        ysq = sb("ysq", [128, TILES, C])
        yss = sb("yss", [128, TILES])
        yvar = sb("yvar", [128, TILES])
        yrstd = sb("yrstd", [128, TILES])
        h1 = [sb(f"h1_{i}", [128, TILES, 2, C]) for i in range(2)]
        h1_t = sb("h1_t", [128, TILES, 128])
        lmax = sb("lmax", [128, TILES])
        lsh = sb("lsh", [128, TILES, EXPERTS])
        ex = sb("ex", [128, TILES, EXPERTS])
        esum = sb("esum", [128, TILES])
        erec = sb("erec", [128, TILES])
        prob = sb("prob", [128, TILES, EXPERTS])
        ge = sb("ge", [128, TILES, EXPERTS, EXPERTS])
        geb = sb("geb", [128, TILES, EXPERTS, EXPERTS])
        gd = sb("gd", [128, TILES, EXPERTS, EXPERTS])
        rank = sb("rank", [128, TILES, EXPERTS])
        top = sb("top", [128, TILES, EXPERTS])
        ptop = sb("ptop", [128, TILES, EXPERTS])
        psum2 = sb("psum2", [128, TILES])
        pguard = sb("pguard", [128, TILES])
        prec = sb("prec", [128, TILES])
        comb = sb("comb", [128, TILES, EXPERTS])
        crest = sb("crest", [128, TILES, EXPERTS])
        crest2 = sb("crest2", [128, TILES, EXPERTS])
        csplit = sb("csplit", [128, TILES, SPLIT, EXPERTS], bf16)
        comb_t = sb("comb_t", [SPLIT * EXPERTS, TILES, 128], bf16)
        hid = sb("hid", [128, PAIRS, CT])
        hids = sb("hids", [128, PAIRS, CT])
        y2 = sb("y2", [128, TILES, C])
        y2sum = sb("y2sum", [128, TILES])
        y2c = sb("y2c", [128, TILES, C])
        y2sq = sb("y2sq", [128, TILES, C])
        y2ss = sb("y2ss", [128, TILES])
        y2var = sb("y2var", [128, TILES])
        y2rstd = sb("y2rstd", [128, TILES])
        ot = [sb(f"ot{i}", [128, TILES, C]) for i in range(2)]

        half = sb("half", [128, TILES * HEADS])
        neghalf = sb("neghalf", [128, TILES])
        euler = sb("euler", [128, TILES * EXPERTS])
        wb_sum = sb("wb_sum", [128, 2 * HEADS])
        wb_c = sb("wb_c", [128, 2, C])
        ident16 = sb("ident16", [128, 128], bf16)
        select16 = sb("select16", [SPLIT * EXPERTS, PAIRS, 128], bf16)
        b2split = sb("b2split", [SPLIT * EXPERTS, SPLIT, C], bf16)
        b2rest = sb("b2rest", [SPLIT * EXPERTS, 2, C])

        bk_up = [ps("bk_up0"), ps("bk_up1")]
        bk_gate = [ps("bk_gate0"), ps("bk_gate1")]
        bk_s1 = ps("bk_s1")
        bk_vec = ps("bk_vec")
        bk_act = ps("bk_act")
        bk_mid = ps("bk_mid")

        f = {name: sem(name) for name in (
            "s_params", "s_consts", "s_wsum", "s_setup", "s_b2a", "s_b2b", "s_b2c", "s_b2d",
            "s1_done", "rows_ready", "t_done", "cols_ready", "q_done", "expand_ready", "d_done", "ht_done",
            "ht_ready", "d_ready", "dsq_ready", "dss_ready", "dvar_ready", "dstd_ready", "dste_ready",
            "drec_ready", "n_ready", "k0_ready", "k_ready", "v0_ready", "v_ready",
            "g_done", "gm_ready", "kv_ready", "y_done", "ysum_ready", "yc_ready", "ysq_ready", "yss_ready",
            "yvar_ready", "yrstd_ready", "h1_ready", "h1t_done", "h1t_ready", "logits_done",
            "lmax_ready", "lsh_ready", "ex_ready", "esum_ready", "erec_ready", "prob_ready", "ge_ready",
            "geb_ready", "gd_ready", "rank_ready", "top_ready", "ptop_ready", "psum2_ready", "pguard_ready",
            "prec_ready", "comb_ready", "chi_ready", "crest_ready", "cmid_ready", "crest2_ready",
            "csplit_ready", "combt_done", "combt_ready", "up_done", "hid_ready", "gate_done", "hids_ready",
            "down_done", "y2_ready", "y2sum_ready", "y2c_ready", "y2sq_ready", "y2ss_ready", "y2var_ready",
            "y2rstd_ready", "ot_ready")}
        x_loaded = [[sem(f"x_loaded{i}{j}") for j in range(2)] for i in range(2)]
        stored = [sem(f"stored{i}") for i in range(2)]

        def F(name):
            return f[name]

        def over(ap, count):
            return ap.unsqueeze(len(ap.shape)).to_broadcast([*ap.shape, count])

        def steps(eng, step):
            step(0, 0, 0, True, False, False)
            step(1, 0, 1, True, True, False)
            for it in range(1, CHUNKS // 2):
                step(it * 2, it, 0, True, True, True)
                step(it * 2 + 1, it, 1, True, True, True)
            step(CHUNKS, CHUNKS // 2, 0, False, True, True)
            step(CHUNKS + 1, CHUNKS // 2, 1, False, False, True)

        block = ctx.enter_context(nc.Block())

        @block.sync
        def _(sp):
            def load(c, par):
                for h in range(2):
                    sp.dma_start(xt[par][:, h * 4:h * 4 + 4, :, :],
                                 x_v[c, :, h * 4:h * 4 + 4, :].rearrange("p n (s w) -> p n s w", s=2)
                                 ).then_inc(x_loaded[par][h], 16)

            def store(c, it, par):
                sp.wait_ge(F("ot_ready"), c + 1)
                sp.dma_start(out_v[c, :, :, :], ot[par][:, :, :]).then_inc(stored[par], 16)

            sp.dma_start(par_sb[:, :], params).then_inc(F("s_params"), 16)
            load(0, 0)
            load(1, 1)
            sp.wait_ge(F("s1_done"), 1)
            load(2, 0)
            sp.wait_ge(F("s1_done"), 2)
            load(3, 1)
            for it in range(1, CHUNKS // 2 - 1):
                for par in range(2):
                    s = it * 2 + par
                    sp.wait_ge(F("s1_done"), s + 1)
                    load(s + 2, par)
                    store(s - 2, it, par)
            for s in range(CHUNKS - 2, CHUNKS + 2):
                store(s - 2, s // 2, s % 2)
            for par in range(2):
                sp.wait_ge(stored[par], 16 * (CHUNKS // 2))

        @block.gpsimd
        def _(pool):
            nc.gpsimd.memset(half[:, :], 0.5)
            nc.gpsimd.memset(neghalf[:, :], -0.5)
            nc.gpsimd.memset(euler[:, :], float(np.e)).then_inc(F("s_consts"), 1)
            pool.wait_ge(F("s_consts"), 1)
            pool.wait_ge(F("s_params"), 16)

            def kv_matrix(c):
                pool.wait_ge(F("gm_ready"), c + 1)
                pool.wait_ge(F("y_done"), c)
                nc.gpsimd.tensor_tensor(kv[:, :, :], gm[:, :, :],
                                        P("twice").unsqueeze(1).to_broadcast([128, TILES, C]),
                                        ALU.add).then_inc(F("kv_ready"), 1)

            def rstd(c, ss, var, out_, ready, mid, done):
                pool.wait_ge(F(ready), c + 1)
                nc.gpsimd.tensor_scalar(var[:, :], ss[:, :], 1.0 / C, 1e-5, ALU.mult, ALU.add).then_inc(F(mid), 1)
                pool.wait_ge(F(mid), c + 1)
                nc.gpsimd.tensor_tensor(out_[:, :], var[:, :], neghalf[:, :], ALU.pow).then_inc(F(done), 1)

            def exponentials(c):
                pool.wait_ge(F("lsh_ready"), c + 1)
                nc.gpsimd.tensor_tensor(ex[:, :, :], euler[:, :].rearrange("p (t e) -> p t e", e=EXPERTS),
                                        lsh[:, :, :], ALU.pow).then_inc(F("ex_ready"), 1)

            def head_std(c):
                pool.wait_ge(F("dss_ready"), c + 1)
                nc.gpsimd.tensor_scalar(dvar[:, :], dss[:, :], 1.0 / (HEAD - 1), 0.0, ALU.mult, ALU.add
                                        ).then_inc(F("dvar_ready"), 1)
                pool.wait_ge(F("dvar_ready"), c + 1)
                nc.gpsimd.tensor_tensor(dstd[:, :], dvar[:, :], half[:, :], ALU.pow).then_inc(F("dstd_ready"), 1)
                pool.wait_ge(F("dstd_ready"), c + 1)
                nc.gpsimd.tensor_scalar(dste[:, :], dstd[:, :], 1.0, 1e-5, ALU.mult, ALU.add
                                        ).then_inc(F("dste_ready"), 1)

            def keys(c):
                pool.wait_ge(F("n_ready"), c + 1)
                pool.wait_ge(F("g_done"), c)
                nc.gpsimd.tensor_tensor(k0[:, :, :], n[:, :, :], P("kw").unsqueeze(1).to_broadcast([128, TILES, C]),
                                        ALU.mult).then_inc(F("k0_ready"), 1)
                pool.wait_ge(F("k0_ready"), c + 1)
                nc.gpsimd.tensor_tensor(k[:, :, :], k0[:, :, :], P("kb").unsqueeze(1).to_broadcast([128, TILES, C]),
                                        ALU.add).then_inc(F("k_ready"), 1)

            def step(s, it, par, front, middle, back):
                if middle:
                    kv_matrix(s - 1)
                    rstd(s - 1, yss, yvar, yrstd, "yss_ready", "yvar_ready", "yrstd_ready")
                    exponentials(s - 1)
                if front:
                    head_std(s)
                    keys(s)
                if back:
                    rstd(s - 2, y2ss, y2var, y2rstd, "y2ss_ready", "y2var_ready", "y2rstd_ready")
            steps(pool, step)

        @block.scalar
        def _(act):
            act.wait_ge(F("s_params"), 16)

            def rows_copy(c):
                act.wait_ge(F("s1_done"), c + 1)
                act.wait_ge(F("t_done"), c)
                nc.scalar.activation(rows[:, :], bk_s1[:, :], ACT.Copy).then_inc(F("rows_ready"), 1)

            def cols_copy(c):
                act.wait_ge(F("t_done"), c + 1)
                act.wait_ge(F("q_done"), c)
                nc.scalar.activation(cols[:, :, :, :, :, :].rearrange("p a b g t i -> p (a b g t i)"),
                                     bk_act[:, :], ACT.Copy).then_inc(F("cols_ready"), 1)

            def square(c, out_, in_, ready, used, done):
                act.wait_ge(F(ready), c + 1)
                act.wait_ge(F(used), c)
                nc.scalar.activation(out_[:, :, :], in_[:, :, :], ACT.Square).then_inc(F(done), 1)

            def gelu(c):
                for q in range(PAIRS):
                    act.wait_ge(F("up_done"), c * PAIRS + q + 1)
                    if q == 0:
                        act.wait_ge(F("hids_ready"), c * PAIRS)
                    nc.scalar.activation(hid[:, q, :], bk_up[q % 2][:, :], ACT.Gelu,
                                         bias=P("b1")[:, q:q + 1]).then_inc(F("hid_ready"), 1)

            def h1t_copy(c):
                act.wait_ge(F("h1t_done"), c + 1)
                act.wait_ge(F("up_done"), c * PAIRS)
                nc.scalar.activation(h1_t[:, :, :].rearrange("p t k -> p (t k)"), bk_act[:, :],
                                     ACT.Copy).then_inc(F("h1t_ready"), 1)

            def combt_copy(c):
                act.wait_ge(F("combt_done"), c + 1)
                act.wait_ge(F("down_done"), c)
                nc.scalar.activation(comb_t[:, :, :].rearrange("p t k -> p (t k)"),
                                     bk_act[0:SPLIT * EXPERTS, 0:CT // 2].bitcast(bf16),
                                     ACT.Copy).then_inc(F("combt_ready"), 1)

            def ht_copy(c):
                act.wait_ge(F("ht_done"), c + 1)
                act.wait_ge(F("y_done"), c)
                nc.scalar.activation(h_t[:, :, :].rearrange("p t k -> p (t k)"), bk_act[:, 0:TILES * TOKENS],
                                     ACT.Identity, bias=P("btok_col")).then_inc(F("ht_ready"), 1)

            def step(s, it, par, front, middle, back):
                if front:
                    rows_copy(s)
                if middle:
                    square(s - 1, ysq, yc, "yc_ready", "yss_ready", "ysq_ready")
                if front:
                    cols_copy(s)
                if back:
                    gelu(s - 2)
                if middle:
                    h1t_copy(s - 1)
                if back:
                    combt_copy(s - 2)
                if front:
                    ht_copy(s)
                    square(s, dsq, d, "d_ready", "dss_ready", "dsq_ready")
                if back:
                    square(s - 2, y2sq, y2c, "y2c_ready", "y2ss_ready", "y2sq_ready")
            steps(act, step)

        @block.vector
        def _(dve):
            dve.wait_ge(F("s_params"), 16)
            wb = par_sb[:, AT["wtok"][0]:AT["btok"][1]]
            nc.vector.reduce_sum(wb_sum[:, :], wb.rearrange("p (g e) -> p g e", e=HEAD), AX.X
                                 ).then_inc(F("s_wsum"), 1)
            nc.vector.tensor_copy(ident16[:, :], P("ident"))
            nc.vector.tensor_copy(select16[:, :, :].rearrange("p q m -> p (q m)"), P("select")[0:SPLIT * EXPERTS, :])
            b2 = P("b2")[0:SPLIT * EXPERTS, :]
            nc.vector.tensor_copy(b2split[:, 0, :], b2).then_inc(F("s_b2a"), 1)
            dve.wait_ge(F("s_b2a"), 1)
            nc.vector.tensor_tensor(b2rest[:, 0, :], b2, b2split[:, 0, :], ALU.subtract).then_inc(F("s_b2b"), 1)
            dve.wait_ge(F("s_b2b"), 1)
            nc.vector.tensor_copy(b2split[:, 1, :], b2rest[:, 0, :]).then_inc(F("s_b2c"), 1)
            dve.wait_ge(F("s_b2c"), 1)
            nc.vector.tensor_tensor(b2rest[:, 1, :], b2rest[:, 0, :], b2split[:, 1, :], ALU.subtract
                                    ).then_inc(F("s_b2d"), 1)
            dve.wait_ge(F("s_b2d"), 1)
            nc.vector.tensor_copy(b2split[:, 2, :], b2rest[:, 1, :])
            dve.wait_ge(F("s_wsum"), 1)
            nc.vector.scalar_tensor_tensor(wb_c[:, :, :].rearrange("p a (g e) -> p (a g) e", e=HEAD),
                                           over(wb_sum[:, :], HEAD), -1.0 / HEAD,
                                           wb.rearrange("p (g e) -> p g e", e=HEAD), ALU.mult, ALU.add
                                           ).then_inc(F("s_setup"), 1)
            dve.wait_ge(F("s_setup"), 1)

            def mask_gram(c):
                dve.wait_ge(F("g_done"), c + 1)
                dve.wait_ge(F("kv_ready"), c)
                nc.vector.tensor_tensor(gm[:, :, :], bk_mid[:, 0:TILES * C].rearrange("p (t e) -> p t e", e=C),
                                        P("headmask").unsqueeze(1).to_broadcast([128, TILES, C]),
                                        ALU.mult).then_inc(F("gm_ready"), 1)

            def norm1_centre(c):
                y = bk_mid[:, 0:TILES * C].rearrange("p (t e) -> p t e", e=C)
                dve.wait_ge(F("y_done"), c + 1)
                nc.vector.reduce_sum(ysum[:, :], y, AX.X).then_inc(F("ysum_ready"), 1)
                dve.wait_ge(F("ysum_ready"), c + 1)
                nc.vector.scalar_tensor_tensor(yc[:, :, :], over(ysum[:, :], C), -1.0 / C, y, ALU.mult, ALU.add
                                               ).then_inc(F("yc_ready"), 1)

            def norm1_sum(c):
                dve.wait_ge(F("ysq_ready"), c + 1)
                nc.vector.reduce_sum(yss[:, :], ysq[:, :, :], AX.X).then_inc(F("yss_ready"), 1)

            def norm1_scale(c, par):
                dve.wait_ge(F("yrstd_ready"), c + 1)
                nc.vector.tensor_tensor(h1[par][:, :, :, :],
                                        yc[:, :, :].unsqueeze(2).to_broadcast([128, TILES, 2, C]),
                                        over(over(yrstd[:, :], 2), C), ALU.mult).then_inc(F("h1_ready"), 1)

            def expand_columns(c):
                dve.wait_ge(F("q_done"), c + 1)
                dve.wait_ge(F("ht_done"), c)
                nc.vector.tensor_tensor(expand[:, :, :, :].rearrange("p n i j -> p (n i) j"),
                                        over(bk_vec[:, 0:CHUNK * GRID], GRID),
                                        P("jmask").unsqueeze(1).to_broadcast([128, CHUNK * GRID, GRID]),
                                        ALU.mult).then_inc(F("expand_ready"), 1)

            def router_shift(c):
                logits = bk_mid[:, 0:TILES * EXPERTS].rearrange("p (t e) -> p t e", e=EXPERTS)
                dve.wait_ge(F("logits_done"), c + 1)
                nc.vector.reduce_max(lmax[:, :], logits, AX.X).then_inc(F("lmax_ready"), 1)
                dve.wait_ge(F("lmax_ready"), c + 1)
                nc.vector.tensor_tensor(lsh[:, :, :], logits, over(lmax[:, :], EXPERTS), ALU.subtract
                                        ).then_inc(F("lsh_ready"), 1)

            def router_probabilities(c):
                dve.wait_ge(F("ex_ready"), c + 1)
                nc.vector.reduce_sum(esum[:, :], ex[:, :, :], AX.X).then_inc(F("esum_ready"), 1)
                dve.wait_ge(F("esum_ready"), c + 1)
                nc.vector.reciprocal(erec[:, :], esum[:, :]).then_inc(F("erec_ready"), 1)
                dve.wait_ge(F("erec_ready"), c + 1)
                nc.vector.tensor_tensor(prob[:, :, :], ex[:, :, :], over(erec[:, :], EXPERTS), ALU.mult
                                        ).then_inc(F("prob_ready"), 1)

            def router_top2(c):
                dve.wait_ge(F("prob_ready"), c + 1)
                nc.vector.tensor_tensor(ge[:, :, :, :],
                                        prob[:, :, :].unsqueeze(2).to_broadcast([128, TILES, EXPERTS, EXPERTS]),
                                        over(prob[:, :, :], EXPERTS), ALU.is_ge).then_inc(F("ge_ready"), 1)
                dve.wait_ge(F("ge_ready"), c + 1)
                nc.vector.tensor_tensor(geb[:, :, :, :].rearrange("p t i j -> p t (i j)"),
                                        ge[:, :, :, :].rearrange("p t i j -> p t (i j)"),
                                        P("before").unsqueeze(1).to_broadcast([128, TILES, EXPERTS * EXPERTS]),
                                        ALU.mult).then_inc(F("geb_ready"), 1)
                dve.wait_ge(F("geb_ready"), c + 1)
                nc.vector.tensor_tensor(gd[:, :, :, :], geb[:, :, :, :],
                                        geb[:, :, :, :].rearrange("p t i j -> p t j i"), ALU.subtract
                                        ).then_inc(F("gd_ready"), 1)
                dve.wait_ge(F("gd_ready"), c + 1)
                nc.vector.reduce_sum(rank[:, :, :], gd[:, :, :, :], AX.X).then_inc(F("rank_ready"), 1)
                dve.wait_ge(F("rank_ready"), c + 1)
                nc.vector.tensor_tensor(top[:, :, :], rank[:, :, :],
                                        P("rank_limit").rearrange("p (t e) -> p t e", e=EXPERTS), ALU.is_le
                                        ).then_inc(F("top_ready"), 1)
                dve.wait_ge(F("top_ready"), c + 1)
                nc.vector.tensor_tensor(ptop[:, :, :], prob[:, :, :], top[:, :, :], ALU.mult
                                        ).then_inc(F("ptop_ready"), 1)

            def router_weights(c):
                dve.wait_ge(F("ptop_ready"), c + 1)
                nc.vector.reduce_sum(psum2[:, :], ptop[:, :, :], AX.X).then_inc(F("psum2_ready"), 1)
                dve.wait_ge(F("psum2_ready"), c + 1)
                nc.vector.tensor_scalar(pguard[:, :], psum2[:, :], 1e-12, None, ALU.max).then_inc(F("pguard_ready"), 1)
                dve.wait_ge(F("pguard_ready"), c + 1)
                nc.vector.reciprocal(prec[:, :], pguard[:, :]).then_inc(F("prec_ready"), 1)
                dve.wait_ge(F("prec_ready"), c + 1)
                nc.vector.tensor_tensor(comb[:, :, :], ptop[:, :, :], over(prec[:, :], EXPERTS), ALU.mult
                                        ).then_inc(F("comb_ready"), 1)

            def router_split(c):
                dve.wait_ge(F("comb_ready"), c + 1)
                dve.wait_ge(F("combt_done"), c)
                nc.vector.tensor_copy(csplit[:, :, 0, :], comb[:, :, :]).then_inc(F("chi_ready"), 1)
                dve.wait_ge(F("chi_ready"), c + 1)
                nc.vector.tensor_tensor(crest[:, :, :], comb[:, :, :], csplit[:, :, 0, :], ALU.subtract
                                        ).then_inc(F("crest_ready"), 1)
                dve.wait_ge(F("crest_ready"), c + 1)
                nc.vector.tensor_copy(csplit[:, :, 1, :], crest[:, :, :]).then_inc(F("cmid_ready"), 1)
                dve.wait_ge(F("cmid_ready"), c + 1)
                nc.vector.tensor_tensor(crest2[:, :, :], crest[:, :, :], csplit[:, :, 1, :], ALU.subtract
                                        ).then_inc(F("crest2_ready"), 1)
                dve.wait_ge(F("crest2_ready"), c + 1)
                nc.vector.tensor_copy(csplit[:, :, 2, :], crest2[:, :, :]).then_inc(F("csplit_ready"), 1)

            def gate(c, q):
                dve.wait_ge(F("gate_done"), c * PAIRS + q + 1)
                dve.wait_ge(F("hid_ready"), c * PAIRS + q + 1)
                if q == 0:
                    dve.wait_ge(F("down_done"), c)
                nc.vector.tensor_tensor(hids[:, q, :], hid[:, q, :], bk_gate[q % 2][:, :], ALU.mult
                                        ).then_inc(F("hids_ready"), 1)

            def head_centred(c):
                dve.wait_ge(F("d_done"), c + 1)
                nc.vector.tensor_tensor(d[:, :, :], bk_vec[:, 0:TILES * C].rearrange("p (t e) -> p t e", e=C),
                                        wb_c[:, 1, :].unsqueeze(1).to_broadcast([128, TILES, C]),
                                        ALU.add).then_inc(F("d_ready"), 1)

            def head_norm(c):
                dve.wait_ge(F("dsq_ready"), c + 1)
                nc.vector.reduce_sum(dss[:, :], dsq[:, :, :].rearrange("p t (g e) -> p (t g) e", e=HEAD), AX.X
                                     ).then_inc(F("dss_ready"), 1)

            def head_scale(c):
                dve.wait_ge(F("dste_ready"), c + 1)
                nc.vector.reciprocal(drec[:, :], dste[:, :]).then_inc(F("drec_ready"), 1)
                dve.wait_ge(F("drec_ready"), c + 1)
                dve.wait_ge(F("k0_ready"), c)
                nc.vector.tensor_tensor(n[:, :, :].rearrange("p t (g e) -> p (t g) e", e=HEAD),
                                        d[:, :, :].rearrange("p t (g e) -> p (t g) e", e=HEAD),
                                        over(drec[:, :], HEAD), ALU.mult).then_inc(F("n_ready"), 1)
                dve.wait_ge(F("n_ready"), c + 1)
                nc.vector.tensor_tensor(v0[:, :, :], n[:, :, :], P("vw").unsqueeze(1).to_broadcast([128, TILES, C]),
                                        ALU.mult).then_inc(F("v0_ready"), 1)
                dve.wait_ge(F("v0_ready"), c + 1)
                dve.wait_ge(F("g_done"), c)
                nc.vector.tensor_tensor(v[:, :, :], v0[:, :, :], P("vb").unsqueeze(1).to_broadcast([128, TILES, C]),
                                        ALU.add).then_inc(F("v_ready"), 1)

            def norm2_centre(c, par):
                dve.wait_ge(F("down_done"), c + 1)
                nc.vector.scalar_tensor_tensor(y2[:, :, :], h1[par][:, :, 0, :], 2.0,
                                               bk_mid[:, 0:TILES * C].rearrange("p (t e) -> p t e", e=C),
                                               ALU.mult, ALU.add).then_inc(F("y2_ready"), 1)
                dve.wait_ge(F("y2_ready"), c + 1)
                nc.vector.reduce_sum(y2sum[:, :], y2[:, :, :], AX.X).then_inc(F("y2sum_ready"), 1)
                dve.wait_ge(F("y2sum_ready"), c + 1)
                nc.vector.scalar_tensor_tensor(y2c[:, :, :], over(y2sum[:, :], C), -1.0 / C, y2[:, :, :],
                                               ALU.mult, ALU.add).then_inc(F("y2c_ready"), 1)

            def norm2_sum(c):
                dve.wait_ge(F("y2sq_ready"), c + 1)
                nc.vector.reduce_sum(y2ss[:, :], y2sq[:, :, :], AX.X).then_inc(F("y2ss_ready"), 1)

            def norm2_scale(c, it, par):
                dve.wait_ge(F("y2rstd_ready"), c + 1)
                dve.wait_ge(stored[par], 16 * (it - 1))
                nc.vector.tensor_tensor(ot[par][:, :, :], y2c[:, :, :], over(y2rstd[:, :], C), ALU.mult
                                        ).then_inc(F("ot_ready"), 1)

            def step(s, it, par, front, middle, back):
                if middle:
                    mask_gram(s - 1)
                    norm1_centre(s - 1)
                    norm1_sum(s - 1)
                if front:
                    expand_columns(s)
                if middle:
                    norm1_scale(s - 1, 1 - par)
                    router_shift(s - 1)
                if back:
                    gate(s - 2, 0)
                    gate(s - 2, 1)
                if front:
                    head_centred(s)
                if middle:
                    router_probabilities(s - 1)
                if back:
                    gate(s - 2, 2)
                    gate(s - 2, 3)
                if front:
                    head_norm(s)
                if middle:
                    router_top2(s - 1)
                    router_weights(s - 1)
                if front:
                    head_scale(s)
                if back:
                    norm2_centre(s - 2, par)
                if middle:
                    router_split(s - 1)
                if back:
                    norm2_sum(s - 2)
                    norm2_scale(s - 2, it, par)
            steps(dve, step)

        @block.tensor
        def _(pe):
            pe.wait_ge(F("s_params"), 16)
            pe.wait_ge(F("s_setup"), 1)
            rows_op = P("rows_op").rearrange("p (s m) -> p s m", s=2)
            cols_op = P("cols_op").rearrange("p (s m) -> p s m", s=2)
            w1 = P("w1").rearrange("p (q m) -> p q m", q=2)
            w2 = P("w2").rearrange("p (q m) -> p q m", q=PAIRS)

            def row_products(c, it, par):
                pe.wait_ge(F("rows_ready"), c)
                for h in range(2):
                    pe.wait_ge(x_loaded[par][h], (it + 1) * 16)
                    for r in range(2):
                        for g in range(2 * h, 2 * h + 2):
                            last = nc.tensor.matmul(bk_s1[g * OPS:(g + 1) * OPS, :].rearrange("p (n w) -> p n w", n=2),
                                                    rows_op[:, r, :], xt[par][:, 2 * g:2 * g + 2, r, :],
                                                    start=(r == 0), stop=(r == 1))
                last.then_inc(F("s1_done"), 1)

            def transpose_rows(c):
                pe.wait_ge(F("rows_ready"), c + 1)
                pe.wait_ge(F("ht_ready"), c)
                for b in range(4):
                    last = nc.tensor.transpose(bk_act[:, b * 128:(b + 1) * 128], rows[:, b * 128:(b + 1) * 128],
                                               P("ident"))
                last.then_inc(F("t_done"), 1)

            def column_products(c):
                pe.wait_ge(F("cols_ready"), c + 1)
                pe.wait_ge(F("d_ready"), c)
                for h in range(2):
                    for t in range(KINDS):
                        last = nc.tensor.matmul(bk_vec[t * OPS:(t + 1) * OPS, 0:CHUNK * GRID]
                                                .rearrange("p (g n i) -> p g n i", g=GROUPS, n=2),
                                                cols_op[:, h, :],
                                                cols[:, :, h, :, t, :].rearrange("p n g i -> p g n i"),
                                                start=(h == 0), stop=(h == 1))
                last.then_inc(F("q_done"), 1)

            def tokens(c):
                pe.wait_ge(F("expand_ready"), c + 1)
                for t in range(TILES):
                    last = nc.tensor.matmul(bk_vec[:, t * C:(t + 1) * C],
                                            expand[:, 2 * t:2 * t + 2, :, :].rearrange("p n i j -> p (n i j)"),
                                            wb_c[:, 0, :], start=True, stop=True)
                last.then_inc(F("d_done"), 1)
                ex_v = expand[:, :, :, :].rearrange("p (t n) i j -> p n t (i j)", n=2)
                for m in range(2):
                    last = nc.tensor.matmul(bk_act[m * C:(m + 1) * C, 0:TILES * TOKENS]
                                            .rearrange("p (t k) -> p t k", t=TILES),
                                            P("wtok"), ex_v[:, m, :, :], start=True, stop=True)
                last.then_inc(F("ht_done"), 1)

            def gram(c):
                pe.wait_ge(F("k_ready"), c + 1)
                pe.wait_ge(F("v_ready"), c + 1)
                for t in range(TILES):
                    for m in range(2):
                        o = slice(m * 64, m * 64 + 64)
                        last = nc.tensor.matmul(bk_mid[o, t * C:(t + 1) * C], k[o, t, :], v[o, t, :],
                                                start=True, stop=True)
                last.then_inc(F("g_done"), 1)

            def attention(c):
                pe.wait_ge(F("kv_ready"), c + 1)
                pe.wait_ge(F("ht_ready"), c + 1)
                for t in range(TILES):
                    for m in range(2):
                        o = slice(m * 64, m * 64 + 64)
                        last = nc.tensor.matmul(bk_mid[o, t * C:(t + 1) * C], h_t[o, t, :], kv[o, t, :],
                                                start=True, stop=True)
                last.then_inc(F("y_done"), 1)

            def transpose_h1(c, par):
                pe.wait_ge(F("h1_ready"), c + 1)
                for t in range(TILES):
                    last = nc.tensor.transpose(bk_act[:, t * 128:(t + 1) * 128], h1[par][:, t, :, :].rearrange("p r e -> p (r e)"),
                                               P("ident"))
                last.then_inc(F("h1t_done"), 1)

            def router(c):
                pe.wait_ge(F("h1t_ready"), c + 1)
                for t in range(TILES):
                    last = nc.tensor.matmul(bk_mid[:, t * EXPERTS:(t + 1) * EXPERTS], h1_t[0:C, t, :],
                                            P("router")[0:C, :], start=True, stop=True)
                last.then_inc(F("logits_done"), 1)

            def up(c):
                for q in range(PAIRS):
                    if q < 2:
                        pe.wait_ge(F("hid_ready"), c * PAIRS)
                    else:
                        pe.wait_ge(F("hid_ready"), c * PAIRS + q - 1)
                    o = slice((q % 2) * C, (q % 2) * C + C)
                    nc.tensor.matmul(bk_up[q % 2][:, :], w1[o, q // 2, :],
                                     h1_t[o, :, :].rearrange("p t k -> p (t k)"),
                                     start=True, stop=True).then_inc(F("up_done"), 1)

            def transpose_weights(c):
                pe.wait_ge(F("csplit_ready"), c + 1)
                for t in range(TILES):
                    last = nc.tensor.transpose(bk_act[0:SPLIT * EXPERTS, t * 64:(t + 1) * 64].bitcast(bf16),
                                               csplit[:, t, :, :].rearrange("p s e -> p (s e)"), ident16[:, :])
                last.then_inc(F("combt_done"), 1)

            def spread(c, q):
                if q == 0:
                    pe.wait_ge(F("combt_ready"), c + 1)
                if q < 2:
                    pe.wait_ge(F("hids_ready"), c * PAIRS)
                else:
                    pe.wait_ge(F("hids_ready"), c * PAIRS + q - 1)
                nc.tensor.matmul(bk_gate[q % 2][:, :], select16[:, q, :], comb_t[:, :, :].rearrange("p t k -> p (t k)"),
                                 start=True, stop=True).then_inc(F("gate_done"), 1)

            def down(c):
                pe.wait_ge(F("hids_ready"), (c + 1) * PAIRS)
                pe.wait_ge(F("lsh_ready"), c + 2)
                for t in range(TILES):
                    o = bk_mid[:, t * C:(t + 1) * C]
                    for b in range(SPLIT):
                        nc.tensor.matmul(o, comb_t[:, t, :], b2split[:, b, :], start=(b == 0), stop=False)
                    for q in range(PAIRS):
                        last = nc.tensor.matmul(o, hids[:, q, t * 128:(t + 1) * 128], w2[:, q, :],
                                                start=False, stop=(q == PAIRS - 1))
                last.then_inc(F("down_done"), 1)

            def step(s, it, par, front, middle, back):
                if middle:
                    if back:
                        pe.wait_ge(F("y2_ready"), s - 2)
                    gram(s - 1)
                if front:
                    row_products(s, it, par)
                if middle:
                    attention(s - 1)
                if front:
                    transpose_rows(s)
                if back:
                    up(s - 2)
                if front:
                    column_products(s)
                if middle:
                    pe.wait_ge(F("cols_ready"), s if not front else s + 1)
                    transpose_h1(s - 1, 1 - par)
                    router(s - 1)
                if back:
                    transpose_weights(s - 2)
                    spread(s - 2, 0)
                    spread(s - 2, 1)
                if front:
                    if back:
                        pe.wait_ge(F("combt_ready"), s - 1)
                    elif middle:
                        pe.wait_ge(F("h1t_ready"), s)
                    tokens(s)
                if back:
                    spread(s - 2, 2)
                    spread(s - 2, 3)
                    if not middle:
                        pe.wait_ge(F("lsh_ready"), s - 1)
                    down(s - 2) if middle else down_last(s - 2)

            def down_last(c):
                pe.wait_ge(F("hids_ready"), (c + 1) * PAIRS)
                for t in range(TILES):
                    o = bk_mid[:, t * C:(t + 1) * C]
                    for b in range(SPLIT):
                        nc.tensor.matmul(o, comb_t[:, t, :], b2split[:, b, :], start=(b == 0), stop=False)
                    for q in range(PAIRS):
                        last = nc.tensor.matmul(o, hids[:, q, t * 128:(t + 1) * 128], w2[:, q, :],
                                                start=False, stop=(q == PAIRS - 1))
                last.then_inc(F("down_done"), 1)

            steps(pe, step)


def resize_operator(size):
    scale = size / GRID
    at = (np.arange(GRID) + 0.5) * scale - 0.5
    w = np.maximum(0.0, 1.0 - np.abs(at[:, None] - np.arange(size)[None, :]) / scale)
    return w / w.sum(axis=1, keepdims=True)


def axis_operator():
    def haar(size, sign):
        m = np.zeros((size // 2, size))
        m[np.arange(size // 2), np.arange(0, size, 2)] = 0.5 ** 0.5
        m[np.arange(size // 2), np.arange(1, size, 2)] = sign * 0.5 ** 0.5
        return m
    low1, high1 = haar(SIDE, 1), haar(SIDE, -1)
    low2, high2 = haar(SIDE // 2, 1) @ low1, haar(SIDE // 2, -1) @ low1
    r1, r2 = resize_operator(SIDE // 2), resize_operator(SIDE // 4)
    return np.concatenate([r1 @ low1, r1 @ high1, r2 @ low2, r2 @ high2]).astype(np.float32)


def kernel(x, L0_tok_W, L0_tok_b, L0_attn_kln_weight, L0_attn_kln_bias, L0_attn_vln_weight, L0_attn_vln_bias,
           L0_ffn_router_w, L0_ffn_w1, L0_ffn_b1, L0_ffn_w2, L0_ffn_b2):
    import concourse.bacc as bacc
    from concourse.bass_utils import run_bass_kernel_spmd

    x = np.ascontiguousarray(x)
    par = np.zeros((128, PARAMS), np.float32)

    def put(name, value, rows=128):
        a, b = AT[name]
        par[:rows, a:b] = np.asarray(value).reshape(rows, b - a)

    op = axis_operator()
    put("rows_op", op.T.reshape(128, 2, OPS))
    put("cols_op", op.T.reshape(2, 128, OPS).transpose(1, 0, 2))
    put("ident", np.eye(128))
    put("jmask", np.tile(np.eye(GRID), (128 // GRID, 1)))
    put("headmask", np.tile(np.kron(np.eye(HEADS), np.ones((HEAD, HEAD))) / TOKENS, (2, 1)))
    put("twice", np.tile(2 * np.eye(C), (2, 1)))
    sel = np.zeros((SPLIT, EXPERTS, PAIRS, 2, FF), np.float32)
    for e in range(EXPERTS):
        sel[:, e, e // 2, e % 2, :] = 1
    put("select", sel, SPLIT * EXPERTS)
    i, j = np.arange(EXPERTS)[:, None], np.arange(EXPERTS)[None, :]
    put("before", np.broadcast_to(j < i, (128, EXPERTS, EXPERTS)))
    put("rank_limit", np.broadcast_to(np.arange(EXPERTS) - (EXPERTS - 1) + 1.5, (128, TILES, EXPERTS)))
    w = np.zeros((KINDS, KINDS, GRID, C), np.float32)
    for m, (a, b) in enumerate(MAPS):
        w[a, b] = np.broadcast_to(np.asarray(L0_tok_W)[m], (GRID, C))
    put("wtok", w)
    put("btok", np.broadcast_to(np.asarray(L0_tok_b), (128, C)))
    put("btok_col", np.tile(np.asarray(L0_tok_b), 2))
    for name, value in (("kw", L0_attn_kln_weight), ("kb", L0_attn_kln_bias), ("vw", L0_attn_vln_weight),
                        ("vb", L0_attn_vln_bias)):
        put(name, np.broadcast_to(np.asarray(value).reshape(C), (128, C)))
    put("w1", np.asarray(L0_ffn_w1).reshape(2, 2, 2, C, FF).transpose(1, 3, 0, 2, 4))
    put("b1", np.asarray(L0_ffn_b1).reshape(PAIRS, 2 * FF).T)
    put("w2", np.asarray(L0_ffn_w2).reshape(PAIRS, 2 * FF, C).transpose(1, 0, 2))
    put("router", np.tile(np.asarray(L0_ffn_router_w).T, (2, 1)))
    put("b2", np.tile(np.asarray(L0_ffn_b2), (SPLIT, 1)), SPLIT * EXPERTS)

    nc = bacc.Bacc("TRN2", target_bir_lowering=False, num_devices=1)
    x_d = nc.dram_tensor("x_dram", x.shape, mybir.dt.float32, kind="ExternalInput").ap()
    p_d = nc.dram_tensor("params_dram", par.shape, mybir.dt.float32, kind="ExternalInput").ap()
    o_d = nc.dram_tensor("out_dram", (IMAGES, TOKENS, C), mybir.dt.float32, kind="ExternalOutput").ap()
    vit_tower_kernel(nc, x_d, p_d, o_d)
    r = run_bass_kernel_spmd(nc, [{"x_dram": x, "params_dram": par}], core_ids=[0])
    return r.results[0]["out_dram"]
```

```python
from contextlib import ExitStack

import numpy as np

import concourse.bass as bass
from concourse import mybir

IMAGES, SIDE = 64, 256
GRID = 8
TOKENS = GRID * GRID
C = 64
HEADS = 8
HEAD = C // HEADS
EXPERTS = 8
FF = 64
KINDS = 4
OPS = KINDS * GRID

CHUNK = 8
CHUNKS = IMAGES // CHUNK
TILES = CHUNK * TOKENS // 128
CT = CHUNK * TOKENS
GROUPS = CHUNK // 2
PAIRS = EXPERTS // 2
SPLIT = 3
NEWTON = 3
RSQRT_MAGIC = 0x5F3759DF

LOW1, HIGH1, LOW2, HIGH2 = range(KINDS)
MAPS = [(LOW2, LOW2), (HIGH2, LOW2), (LOW2, HIGH2), (HIGH2, HIGH2),
        (HIGH1, LOW1), (LOW1, HIGH1), (HIGH1, HIGH1)]


def layout(fields):
    at, end = {}, 0
    for name, width in fields:
        at[name] = (end, end + width)
        end += width
    return at, end


FIRST_AT, FIRST = layout([("rows_op", 2 * OPS), ("cols_op", 2 * OPS), ("ident", 128)])
MAIN_AT, MAIN = layout([
    ("jmask", GRID), ("wtok", C), ("btok_col", 1), ("head_centre", C), ("kw", C), ("kb", C), ("vw", C), ("vb", C),
    ("headmask", C), ("twice", C), ("w1", PAIRS * 128), ("router", EXPERTS), ("twice_centre", C),
    ("b1", PAIRS), ("w2", PAIRS * C), ("before", EXPERTS * EXPERTS), ("rank_limit", TILES * EXPERTS)])
PART_AT, PART = layout([("b2", C), ("select", PAIRS * 128)])
PARTS = SPLIT * EXPERTS


def vit_tower_kernel(nc, x, first, main, part, out):
    fp32, bf16, fp32r, i32 = mybir.dt.float32, mybir.dt.bfloat16, mybir.dt.float32r, mybir.dt.int32
    ALU, ACT, AX = mybir.AluOpType, mybir.ActivationFunctionType, mybir.AxisListType

    x_v = x.rearrange("(c n) one (p s) w -> c p n (one s w)", n=CHUNK, s=2)
    out_v = out.rearrange("(c t two) k w -> c (two k) t w", t=TILES, two=2)

    with ExitStack() as ctx:
        def sb(name, shape, dt=fp32):
            return ctx.enter_context(nc.sbuf_tensor(name, shape, dt))

        def ps(name):
            return ctx.enter_context(nc.psum_tensor(name, [128, 512], fp32))

        def sem(name):
            return ctx.enter_context(nc.semaphore(name))

        first_sb = sb("first_sb", [128, FIRST])
        main_sb = sb("main_sb", [128, MAIN])
        part_sb = sb("part_sb", [PARTS, PART])

        def P(name):
            for tile, at in ((first_sb, FIRST_AT), (main_sb, MAIN_AT), (part_sb, PART_AT)):
                if name in at:
                    return tile[:, at[name][0]:at[name][1]]

        def over(ap, count):
            return ap.unsqueeze(len(ap.shape)).to_broadcast([*ap.shape, count])

        def per_tile(name):
            return P(name).unsqueeze(1).to_broadcast([128, TILES, C])

        small, groups = [128, TILES, EXPERTS], [128, TILES * HEADS]
        xt = [sb(f"xt{i}", [128, CHUNK, 2, SIDE]) for i in range(2)]
        rows = sb("rows", [128, 512])
        cols = sb("cols", [128, 2, 2, GROUPS, KINDS, GRID])
        expand = sb("expand", [128, CHUNK, GRID, GRID])
        h_t = sb("h_t", [128, TILES, TOKENS])
        dsq = sb("dsq", [128, TILES, C])
        dss, dvar, dhalf, dstd, dste, drec = (sb(f"d_{x}", groups) for x in ("ss", "var", "half", "std", "ste", "rec"))
        dnewton = [sb(f"d_newton{i}", groups) for i in range(NEWTON + 1)]
        dtmp = [sb(f"d_tmp{i}", groups) for i in range(3)]
        n, k0, v0, k, v = (sb(x, [128, TILES, C]) for x in ("n", "k0", "v0", "k", "v"))
        gm, kv = sb("gm", [128, TILES, C]), sb("kv", [128, TILES, C])
        yc, ysq = sb("yc", [128, TILES, C]), sb("ysq", [128, TILES, C])
        ysum, yss, yvar, yrstd = (sb(f"y_{x}", [128, TILES]) for x in ("sum", "ss", "var", "rstd"))
        h1 = sb("h1", [128, TILES, 2, C])
        h1_t = [sb(f"h1_t{i}", [128, CT], fp32r) for i in range(2)]
        lmax = sb("lmax", [128, TILES])
        lsh, ztop, arg, th = (sb(x, small) for x in ("lsh", "ztop", "arg", "th"))
        ge, geb, gd = (sb(x, [128, TILES, EXPERTS, EXPERTS]) for x in ("ge", "geb", "gd"))
        rank, top, comb, crest, crest2 = (sb(x, small) for x in ("rank", "top", "comb", "crest", "crest2"))
        zsum = sb("zsum", [128, TILES])
        csplit = sb("csplit", [128, TILES, SPLIT, EXPERTS], bf16)
        comb_t = sb("comb_t", [PARTS, CT], bf16)
        hid = sb("hid", [128, PAIRS, CT])
        hids = sb("hids", [128, PAIRS, CT])
        y2t = sb("y2t", [128, CT // 2])
        y2sq = sb("y2sq", [128, TILES, C])
        y2ss, y2var, y2rstd = (sb(f"y2_{x}", [128, TILES]) for x in ("ss", "var", "rstd"))
        ot = [sb(f"ot{i}", [128, TILES, C]) for i in range(2)]

        neghalf = sb("neghalf", [128, TILES])
        ident16 = sb("ident16", [128, 128], bf16)
        select16 = sb("select16", [PARTS, PAIRS, 128], bf16)
        b2sum, b2half, b2c = sb("b2sum", [PARTS, 1]), sb("b2half", [PARTS, C]), sb("b2c", [PARTS, C])
        b2split = sb("b2split", [PARTS, SPLIT, C], bf16)
        b2rest = sb("b2rest", [PARTS, 2, C])
        w1s = sb("w1s", [128, 2, PAIRS, 128], fp32r)
        routers = sb("routers", [128, 2, EXPERTS], fp32r)
        twice_c = sb("twice_c", [128, C], fp32r)
        w2sum, w2c = sb("w2sum", [128, PAIRS]), sb("w2c", [128, PAIRS, C])

        bk_up = [ps("bk_up0"), ps("bk_up1")]
        bk_gate = [ps("bk_gate0"), ps("bk_gate1")]
        bk_act = ps("bk_act")
        bk_vec = ps("bk_vec")
        bk_d = ps("bk_d")
        bk_y2 = ps("bk_y2")

        sems = {}

        def F(name):
            if name not in sems:
                sems[name] = sem(name)
            return sems[name]

        x_loaded = [[sem(f"x_loaded{i}{j}") for j in range(2)] for i in range(2)]
        stored = [sem(f"stored{i}") for i in range(2)]

        def steps(eng, step):
            step(0, 0, 0, True, False, False)
            step(1, 0, 1, True, True, False)
            for it in range(1, CHUNKS // 2):
                step(it * 2, it, 0, True, True, True)
                step(it * 2 + 1, it, 1, True, True, True)
            step(CHUNKS, CHUNKS // 2, 0, False, True, True)
            step(CHUNKS + 1, CHUNKS // 2, 1, False, False, True)

        def tiles_of(bank):
            return bank[:, 0:TILES * C].rearrange("p (t e) -> p t e", e=C)

        block = ctx.enter_context(nc.Block())

        @block.sync
        def _(sp):
            def load(c, par):
                for h in range(2):
                    sp.dma_start(xt[par][:, h * 4:h * 4 + 4, :, :],
                                 x_v[c, :, h * 4:h * 4 + 4, :].rearrange("p n (s w) -> p n s w", s=2)
                                 ).then_inc(x_loaded[par][h], 16)

            def store(c, par):
                sp.wait_ge(F("ot_ready"), c + 1)
                sp.dma_start(out_v[c, :, :, :], ot[par][:, :, :]).then_inc(stored[par], 16)

            sp.dma_start(first_sb[:, :], first).then_inc(F("s_first"), 16)
            load(0, 0)
            sp.dma_start(main_sb[:, :], main).then_inc(F("s_main"), 16)
            sp.dma_start(part_sb[:, :], part).then_inc(F("s_part"), 16)
            load(1, 1)
            sp.wait_ge(F("s1_done"), 1)
            load(2, 0)
            sp.wait_ge(F("s1_done"), 2)
            load(3, 1)
            for it in range(1, CHUNKS // 2 - 1):
                for par in range(2):
                    s = it * 2 + par
                    sp.wait_ge(F("s1_done"), s + 1)
                    load(s + 2, par)
                    store(s - 2, par)
            for s in range(CHUNKS - 2, CHUNKS + 2):
                store(s - 2, s % 2)
            for par in range(2):
                sp.wait_ge(stored[par], 16 * (CHUNKS // 2))

        @block.gpsimd
        def _(pool):
            tt, ts = nc.gpsimd.tensor_tensor, nc.gpsimd.tensor_scalar
            nc.gpsimd.memset(neghalf[:, :], -0.5).then_inc(F("s_consts"), 1)
            pool.wait_ge(F("s_consts"), 1)
            pool.wait_ge(F("s_main"), 16)

            def kv_matrix(c):
                pool.wait_ge(F("gm_ready"), c + 1)
                pool.wait_ge(F("y_done"), c)
                tt(kv[:, :, :], gm[:, :, :], per_tile("twice"), ALU.add).then_inc(F("kv_ready"), 1)

            def rstd(c, ss, var, out_, ready, mid, done):
                pool.wait_ge(F(ready), c + 1)
                ts(var[:, :], ss[:, :], 1.0 / C, 1e-5, ALU.mult, ALU.add).then_inc(F(mid), 1)
                pool.wait_ge(F(mid), c + 1)
                tt(out_[:, :], var[:, :], neghalf[:, :], ALU.pow).then_inc(F(done), 1)

            def head_std(c):
                pool.wait_ge(F("dguess_ready"), c + 1)
                ts(dhalf[:, :], dvar[:, :], -0.5, 0.0, ALU.mult, ALU.add).then_inc(F("dhalf_ready"), 1)
                pool.wait_ge(F("dhalf_ready"), c + 1)
                for i in range(NEWTON):
                    y = dnewton[i]
                    tt(dtmp[0][:, :], y[:, :], dhalf[:, :], ALU.mult).then_inc(F(f"dn_a{i}"), 1)
                    pool.wait_ge(F(f"dn_a{i}"), c + 1)
                    tt(dtmp[1][:, :], dtmp[0][:, :], y[:, :], ALU.mult).then_inc(F(f"dn_b{i}"), 1)
                    pool.wait_ge(F(f"dn_b{i}"), c + 1)
                    ts(dtmp[2][:, :], dtmp[1][:, :], 1.0, 1.5, ALU.mult, ALU.add).then_inc(F(f"dn_c{i}"), 1)
                    pool.wait_ge(F(f"dn_c{i}"), c + 1)
                    tt(dnewton[i + 1][:, :], dtmp[2][:, :], y[:, :], ALU.mult).then_inc(F(f"dn_d{i}"), 1)
                    pool.wait_ge(F(f"dn_d{i}"), c + 1)
                tt(dstd[:, :], dvar[:, :], dnewton[NEWTON][:, :], ALU.mult).then_inc(F("dstd_ready"), 1)
                pool.wait_ge(F("dstd_ready"), c + 1)
                ts(dste[:, :], dstd[:, :], 1.0, 1e-5, ALU.mult, ALU.add).then_inc(F("dste_ready"), 1)

            def keys_values(c):
                pool.wait_ge(F("n_ready"), c + 1)
                pool.wait_ge(F("g_done"), c)
                tt(k0[:, :, :], n[:, :, :], per_tile("kw"), ALU.mult).then_inc(F("k0_ready"), 1)
                tt(v0[:, :, :], n[:, :, :], per_tile("vw"), ALU.mult).then_inc(F("v0_ready"), 1)
                pool.wait_ge(F("k0_ready"), c + 1)
                tt(k[:, :, :], k0[:, :, :], per_tile("kb"), ALU.add).then_inc(F("k_ready"), 1)
                pool.wait_ge(F("v0_ready"), c + 1)
                tt(v[:, :, :], v0[:, :, :], per_tile("vb"), ALU.add).then_inc(F("v_ready"), 1)

            def rank_matrix(c):
                pool.wait_ge(F("ge_ready"), c + 1)
                tt(geb[:, :, :, :].rearrange("p t i j -> p t (i j)"), ge[:, :, :, :].rearrange("p t i j -> p t (i j)"),
                   P("before").unsqueeze(1).to_broadcast([128, TILES, EXPERTS * EXPERTS]), ALU.mult
                   ).then_inc(F("geb_ready"), 1)
                pool.wait_ge(F("geb_ready"), c + 1)
                tt(gd[:, :, :, :], geb[:, :, :, :], geb[:, :, :, :].rearrange("p t i j -> p t j i"), ALU.subtract
                   ).then_inc(F("gd_ready"), 1)

            def split_weights(c):
                pool.wait_ge(F("comb_ready"), c + 1)
                pool.wait_ge(F("combt_done"), c)
                nc.gpsimd.tensor_copy(csplit[:, :, 0, :], comb[:, :, :]).then_inc(F("chi_ready"), 1)
                pool.wait_ge(F("chi_ready"), c + 1)
                tt(crest[:, :, :], comb[:, :, :], csplit[:, :, 0, :], ALU.subtract).then_inc(F("crest_ready"), 1)
                pool.wait_ge(F("crest_ready"), c + 1)
                nc.gpsimd.tensor_copy(csplit[:, :, 1, :], crest[:, :, :]).then_inc(F("cmid_ready"), 1)
                pool.wait_ge(F("cmid_ready"), c + 1)
                tt(crest2[:, :, :], crest[:, :, :], csplit[:, :, 1, :], ALU.subtract).then_inc(F("crest2_ready"), 1)
                pool.wait_ge(F("crest2_ready"), c + 1)
                nc.gpsimd.tensor_copy(csplit[:, :, 2, :], crest2[:, :, :]).then_inc(F("csplit_ready"), 1)

            def step(s, it, par, front, middle, back):
                if middle:
                    kv_matrix(s - 1)
                    rstd(s - 1, yss, yvar, yrstd, "yss_ready", "yvar_ready", "yrstd_ready")
                if front:
                    head_std(s)
                    keys_values(s)
                if middle:
                    rank_matrix(s - 1)
                if back:
                    rstd(s - 2, y2ss, y2var, y2rstd, "y2ss_ready", "y2var_ready", "y2rstd_ready")
                if middle:
                    split_weights(s - 1)
            steps(pool, step)

        @block.scalar
        def _(act):
            act.wait_ge(F("s_main"), 16)

            def rows_copy(c):
                act.wait_ge(F("s1_done"), c + 1)
                act.wait_ge(F("t_done"), c)
                nc.scalar.activation(rows[:, :], bk_act[:, :], ACT.Copy).then_inc(F("rows_ready"), 1)

            def cols_copy(c):
                act.wait_ge(F("t_done"), c + 1)
                act.wait_ge(F("q_done"), c)
                nc.scalar.activation(cols[:, :, :, :, :, :].rearrange("p a b g t i -> p (a b g t i)"),
                                     bk_act[:, :], ACT.Copy).then_inc(F("cols_ready"), 1)

            def square(c, out_, in_, ready, used, done):
                act.wait_ge(F(ready), c + 1)
                act.wait_ge(F(used), c)
                nc.scalar.activation(out_[:, :, :], in_, ACT.Square).then_inc(F(done), 1)

            def gelu(c, q):
                act.wait_ge(F("up_done"), c * PAIRS + q + 1)
                if q == 0:
                    act.wait_ge(F("hids_ready"), c * PAIRS)
                nc.scalar.activation(hid[:, q, :], bk_up[q % 2][:, :], ACT.Gelu,
                                     bias=P("b1")[:, q:q + 1]).then_inc(F("hid_ready"), 1)

            def h1t_upper(c, par):
                act.wait_ge(F("h1t_done"), c + 1)
                nc.scalar.activation(h1_t[par][:, :], bk_gate[0][:, :], ACT.Copy).then_inc(F("h1t_upper"), 1)

            def combt_copy(c):
                act.wait_ge(F("combt_done"), c + 1)
                act.wait_ge(F("down_done"), c)
                nc.scalar.activation(comb_t[:, :], bk_act[0:PARTS, 0:CT // 2].bitcast(bf16),
                                     ACT.Copy).then_inc(F("combt_ready"), 1)

            def ht_copy(c):
                act.wait_ge(F("ht_done"), c + 1)
                act.wait_ge(F("y_done"), c)
                nc.scalar.activation(h_t[:, :, :].rearrange("p t k -> p (t k)"), bk_act[:, 0:TILES * TOKENS],
                                     ACT.Identity, bias=P("btok_col")).then_inc(F("ht_ready"), 1)

            def tanh(c):
                act.wait_ge(F("arg_ready"), c + 1)
                act.wait_ge(F("comb_ready"), c)
                nc.scalar.activation(th[:, :, :], arg[:, :, :], ACT.Tanh).then_inc(F("th_ready"), 1)

            def y2t_copy(c):
                act.wait_ge(F("down_done"), c + 1)
                act.wait_ge(F("back_done"), c)
                nc.scalar.activation(y2t[:, :], bk_act[:, 0:CT // 2], ACT.Copy).then_inc(F("y2t_ready"), 1)

            def step(s, it, par, front, middle, back):
                if front:
                    rows_copy(s)
                if back:
                    gelu(s - 2, 0)
                    gelu(s - 2, 1)
                if front:
                    cols_copy(s)
                if back:
                    combt_copy(s - 2)
                    gelu(s - 2, 2)
                    gelu(s - 2, 3)
                if front:
                    ht_copy(s)
                if middle:
                    square(s - 1, ysq, yc[:, :, :], "yc_ready", "yss_ready", "ysq_ready")
                if front:
                    square(s, dsq, tiles_of(bk_d), "d_done", "dss_ready", "dsq_ready")
                if back:
                    y2t_copy(s - 2)
                if middle:
                    h1t_upper(s - 1, 1 - par)
                if back:
                    square(s - 2, y2sq, tiles_of(bk_y2), "back_done", "y2ss_ready", "y2sq_ready")
                if middle:
                    tanh(s - 1)
            steps(act, step)

        @block.vector
        def _(dve):
            tt, stt, ts = nc.vector.tensor_tensor, nc.vector.scalar_tensor_tensor, nc.vector.tensor_scalar
            rsum, copy = nc.vector.reduce_sum, nc.vector.tensor_copy
            dve.wait_ge(F("s_first"), 16)
            copy(ident16[:, :], P("ident"))
            dve.wait_ge(F("s_main"), 16)
            copy(w1s[:, 0, :, :].rearrange("p q m -> p (q m)"), P("w1")).then_inc(F("s_w1"), 1)
            copy(routers[:, 0, :], P("router"))
            copy(twice_c[:, :], P("twice_centre")).then_inc(F("s_router"), 1)
            w2 = P("w2").rearrange("p (q e) -> p q e", e=C)
            rsum(w2sum[:, :], w2, AX.X).then_inc(F("s_w2"), 1)
            dve.wait_ge(F("s_part"), 16)
            rsum(b2sum[:, :], P("b2"), AX.X)
            ts(b2half[:, :], P("b2"), 0.5, None, ALU.mult).then_inc(F("s_b2"), 1)
            copy(select16[:, :, :].rearrange("p q m -> p (q m)"), P("select"))
            dve.wait_ge(F("s_w1"), 1)
            tt(w1s[:, 1, :, :].rearrange("p q m -> p (q m)"), P("w1"),
               w1s[:, 0, :, :].rearrange("p q m -> p (q m)").bitcast(fp32), ALU.subtract)
            dve.wait_ge(F("s_router"), 1)
            tt(routers[:, 1, :], P("router"), routers[:, 0, :].bitcast(fp32), ALU.subtract)
            dve.wait_ge(F("s_w2"), 1)
            stt(w2c[:, :, :], over(w2sum[:, :], C), -1.0 / C, w2, ALU.mult, ALU.add)
            dve.wait_ge(F("s_b2"), 1)
            stt(b2c[:, :], b2sum[:, :].to_broadcast([PARTS, C]), -0.5 / C, b2half[:, :], ALU.mult, ALU.add
                ).then_inc(F("s_b2c"), 1)
            dve.wait_ge(F("s_b2c"), 1)
            copy(b2split[:, 0, :], b2c[:, :]).then_inc(F("s_b2d"), 1)
            dve.wait_ge(F("s_b2d"), 1)
            tt(b2rest[:, 0, :], b2c[:, :], b2split[:, 0, :], ALU.subtract).then_inc(F("s_b2e"), 1)
            dve.wait_ge(F("s_b2e"), 1)
            copy(b2split[:, 1, :], b2rest[:, 0, :]).then_inc(F("s_b2f"), 1)
            dve.wait_ge(F("s_b2f"), 1)
            tt(b2rest[:, 1, :], b2rest[:, 0, :], b2split[:, 1, :], ALU.subtract).then_inc(F("s_b2g"), 1)
            dve.wait_ge(F("s_b2g"), 1)
            copy(b2split[:, 2, :], b2rest[:, 1, :]).then_inc(F("s_setup"), 1)

            def mask_gram(c):
                dve.wait_ge(F("g_done"), c + 1)
                dve.wait_ge(F("kv_ready"), c)
                tt(gm[:, :, :], tiles_of(bk_vec), per_tile("headmask"), ALU.mult).then_inc(F("gm_ready"), 1)

            def norm1_centre(c):
                dve.wait_ge(F("y_done"), c + 1)
                rsum(ysum[:, :], tiles_of(bk_vec), AX.X).then_inc(F("ysum_ready"), 1)
                dve.wait_ge(F("ysum_ready"), c + 1)
                stt(yc[:, :, :], over(ysum[:, :], C), -1.0 / C, tiles_of(bk_vec), ALU.mult, ALU.add
                    ).then_inc(F("yc_ready"), 1)

            def norm1_sum(c):
                dve.wait_ge(F("ysq_ready"), c + 1)
                rsum(yss[:, :], ysq[:, :, :], AX.X).then_inc(F("yss_ready"), 1)

            def norm1_scale(c):
                dve.wait_ge(F("yrstd_ready"), c + 1)
                dve.wait_ge(F("h1t_done"), c)
                tt(h1[:, :, :, :], yc[:, :, :].unsqueeze(2).to_broadcast([128, TILES, 2, C]),
                   over(over(yrstd[:, :], 2), C), ALU.mult).then_inc(F("h1_ready"), 1)

            def h1t_lower(c, par):
                dve.wait_ge(F("h1t_upper"), c + 1)
                tt(h1_t[par][C:, :], bk_gate[0][C:, :], h1_t[par][C:, :].bitcast(fp32), ALU.subtract
                   ).then_inc(F("h1t_ready"), 1)

            def expand_columns(c):
                dve.wait_ge(F("q_done"), c + 1)
                dve.wait_ge(F("ht_done"), c)
                tt(expand[:, :, :, :].rearrange("p n i j -> p (n i) j"), over(bk_vec[:, 0:CHUNK * GRID], GRID),
                   P("jmask").unsqueeze(1).to_broadcast([128, CHUNK * GRID, GRID]), ALU.mult
                   ).then_inc(F("expand_ready"), 1)

            def router_compare(c):
                logits = bk_vec[:, 0:TILES * EXPERTS].rearrange("p (t e) -> p t e", e=EXPERTS)
                dve.wait_ge(F("logits_done"), c + 1)
                nc.vector.reduce_max(lmax[:, :], logits, AX.X).then_inc(F("lmax_ready"), 1)
                dve.wait_ge(F("lmax_ready"), c + 1)
                tt(lsh[:, :, :], logits, over(lmax[:, :], EXPERTS), ALU.subtract).then_inc(F("lsh_ready"), 1)
                dve.wait_ge(F("lsh_ready"), c + 1)
                tt(ge[:, :, :, :], lsh[:, :, :].unsqueeze(2).to_broadcast([128, TILES, EXPERTS, EXPERTS]),
                   over(lsh[:, :, :], EXPERTS), ALU.is_ge).then_inc(F("ge_ready"), 1)

            def router_top2(c):
                dve.wait_ge(F("gd_ready"), c + 1)
                rsum(rank[:, :, :], gd[:, :, :, :], AX.X).then_inc(F("rank_ready"), 1)
                dve.wait_ge(F("rank_ready"), c + 1)
                tt(top[:, :, :], rank[:, :, :], P("rank_limit").rearrange("p (t e) -> p t e", e=EXPERTS), ALU.is_le
                   ).then_inc(F("top_ready"), 1)

                dve.wait_ge(F("top_ready"), c + 1)
                tt(ztop[:, :, :], lsh[:, :, :], top[:, :, :], ALU.mult).then_inc(F("ztop_ready"), 1)
                dve.wait_ge(F("ztop_ready"), c + 1)
                rsum(zsum[:, :], ztop[:, :, :], AX.X).then_inc(F("zsum_ready"), 1)
                dve.wait_ge(F("zsum_ready"), c + 1)
                dve.wait_ge(F("th_ready"), c)
                stt(arg[:, :, :], over(zsum[:, :], EXPERTS), -0.5, lsh[:, :, :], ALU.mult, ALU.add
                    ).then_inc(F("arg_ready"), 1)

            def router_weights(c):
                dve.wait_ge(F("th_ready"), c + 1)
                dve.wait_ge(F("crest_ready"), c)
                stt(comb[:, :, :], th[:, :, :], 1.0, top[:, :, :], ALU.add, ALU.mult).then_inc(F("comb_ready"), 1)

            def gate(c, q):
                dve.wait_ge(F("gate_done"), c * PAIRS + q + 1)
                dve.wait_ge(F("hid_ready"), c * PAIRS + q + 1)
                if q == 0:
                    dve.wait_ge(F("down_done"), c)
                tt(hids[:, q, :], hid[:, q, :], bk_gate[q % 2][:, :], ALU.mult).then_inc(F("hids_ready"), 1)

            def head_variance(c):
                dve.wait_ge(F("dsq_ready"), c + 1)
                rsum(dss[:, :], dsq[:, :, :].rearrange("p t (g e) -> p (t g) e", e=HEAD), AX.X
                     ).then_inc(F("dss_ready"), 1)
                dve.wait_ge(F("dss_ready"), c + 1)
                dve.wait_ge(F("dstd_ready"), c)
                ts(dvar[:, :], dss[:, :], 1.0 / (HEAD - 1), None, ALU.mult).then_inc(F("dvar_ready"), 1)
                dve.wait_ge(F("dvar_ready"), c + 1)
                ts(dnewton[0][:, :].bitcast(i32), dvar[:, :].bitcast(i32), -0.5, float(RSQRT_MAGIC), ALU.mult, ALU.add
                   ).then_inc(F("dguess_ready"), 1)

            def head_scale(c):
                dve.wait_ge(F("dste_ready"), c + 1)
                nc.vector.reciprocal(drec[:, :], dste[:, :]).then_inc(F("drec_ready"), 1)
                dve.wait_ge(F("drec_ready"), c + 1)
                dve.wait_ge(F("v0_ready"), c)
                tt(n[:, :, :].rearrange("p t (g e) -> p (t g) e", e=HEAD),
                   bk_d[:, 0:TILES * C].rearrange("p (g e) -> p g e", e=HEAD),
                   over(drec[:, :], HEAD), ALU.mult).then_inc(F("n_ready"), 1)

            def norm2_sum(c):
                dve.wait_ge(F("y2sq_ready"), c + 1)
                rsum(y2ss[:, :], y2sq[:, :, :], AX.X).then_inc(F("y2ss_ready"), 1)

            def norm2_scale(c, it, par):
                dve.wait_ge(F("y2rstd_ready"), c + 1)
                dve.wait_ge(stored[par], 16 * (it - 1))
                tt(ot[par][:, :, :], tiles_of(bk_y2), over(y2rstd[:, :], C), ALU.mult).then_inc(F("ot_ready"), 1)

            def step(s, it, par, front, middle, back):
                if middle:
                    mask_gram(s - 1)
                if front:
                    expand_columns(s)
                if back:
                    gate(s - 2, 0)
                    gate(s - 2, 1)
                if middle:
                    norm1_centre(s - 1)
                    norm1_sum(s - 1)
                if back:
                    gate(s - 2, 2)
                    gate(s - 2, 3)
                if front:
                    head_variance(s)
                if middle:
                    norm1_scale(s - 1)
                if front:
                    head_scale(s)
                if middle:
                    h1t_lower(s - 1, 1 - par)
                    router_compare(s - 1)
                if back:
                    norm2_sum(s - 2)
                if middle:
                    router_top2(s - 1)
                if back:
                    norm2_scale(s - 2, it, par)
                if middle:
                    router_weights(s - 1)
            steps(dve, step)

        @block.tensor
        def _(pe):
            pe.wait_ge(F("s_first"), 16)
            rows_op = P("rows_op").rearrange("p (s m) -> p s m", s=2)
            cols_op = P("cols_op").rearrange("p (s m) -> p s m", s=2)

            def row_products(c, it, par):
                for h in range(2):
                    pe.wait_ge(x_loaded[par][h], (it + 1) * 16)
                for r in range(2):
                    for g in range(GROUPS):
                        last = nc.tensor.matmul(bk_act[g * OPS:(g + 1) * OPS, :].rearrange("p (n w) -> p n w", n=2),
                                                rows_op[:, r, :], xt[par][:, 2 * g:2 * g + 2, r, :],
                                                start=(r == 0), stop=(r == 1))
                last.then_inc(F("s1_done"), 1)

            def transpose_rows(c):
                pe.wait_ge(F("rows_ready"), c + 1)
                for b in range(4):
                    last = nc.tensor.transpose(bk_act[:, b * 128:(b + 1) * 128], rows[:, b * 128:(b + 1) * 128],
                                               P("ident"))
                last.then_inc(F("t_done"), 1)

            def column_products(c):
                pe.wait_ge(F("cols_ready"), c + 1)
                for h in range(2):
                    for t in range(KINDS):
                        last = nc.tensor.matmul(bk_vec[t * OPS:(t + 1) * OPS, 0:CHUNK * GRID]
                                                .rearrange("p (g n i) -> p g n i", g=GROUPS, n=2),
                                                cols_op[:, h, :],
                                                cols[:, :, h, :, t, :].rearrange("p n g i -> p g n i"),
                                                start=(h == 0), stop=(h == 1))
                last.then_inc(F("q_done"), 1)

            def tokens(c):
                pe.wait_ge(F("expand_ready"), c + 1)
                ex_v = expand[:, :, :, :].rearrange("p (t n) i j -> p n t (i j)", n=2)
                for m in range(2):
                    last = nc.tensor.matmul(bk_act[m * C:(m + 1) * C, 0:TILES * TOKENS]
                                            .rearrange("p (t k) -> p t k", t=TILES),
                                            P("wtok"), ex_v[:, m, :, :], start=True, stop=True)
                last.then_inc(F("ht_done"), 1)

            def by_image(bank, lhs, rhs, done):
                for t in range(TILES):
                    for m in range(2):
                        o = slice(m * 64, m * 64 + 64)
                        last = nc.tensor.matmul(bank[o, t * C:(t + 1) * C], lhs(o, t), rhs(o, t), start=True, stop=True)
                last.then_inc(F(done), 1)

            def head_centred(c):
                pe.wait_ge(F("ht_ready"), c + 1)
                pe.wait_ge(F("n_ready"), c)
                by_image(bk_d, lambda o, t: h_t[o, t, :], lambda o, t: P("head_centre")[o, :], "d_done")

            def gram(c):
                pe.wait_ge(F("lsh_ready"), c)
                pe.wait_ge(F("k_ready"), c + 1)
                pe.wait_ge(F("v_ready"), c + 1)
                by_image(bk_vec, lambda o, t: k[o, t, :], lambda o, t: v[o, t, :], "g_done")

            def attention(c):
                pe.wait_ge(F("kv_ready"), c + 1)
                by_image(bk_vec, lambda o, t: h_t[o, t, :], lambda o, t: kv[o, t, :], "y_done")

            def transpose_h1(c):
                pe.wait_ge(F("h1_ready"), c + 1)
                for t in range(TILES):
                    last = nc.tensor.transpose(bk_gate[0][:, t * 128:(t + 1) * 128],
                                               h1[:, t, :, :].rearrange("p r e -> p (r e)"), P("ident"))
                last.then_inc(F("h1t_done"), 1)

            def router(c, par):
                pe.wait_ge(F("h1t_ready"), c + 1)
                for t in range(TILES):
                    for b in range(2):
                        last = nc.tensor.matmul(bk_vec[:, t * EXPERTS:(t + 1) * EXPERTS],
                                                h1_t[par][:, t * 128:(t + 1) * 128], routers[:, b, :],
                                                start=(b == 0), stop=(b == 1))
                last.then_inc(F("logits_done"), 1)

            def up(c, q, par):
                if q < 2:
                    pe.wait_ge(F("hid_ready"), c * PAIRS)
                else:
                    pe.wait_ge(F("hid_ready"), c * PAIRS + q - 1)
                for b in range(2):
                    last = nc.tensor.matmul(bk_up[q % 2][:, :], w1s[:, b, q, :], h1_t[par][:, :],
                                            start=(b == 0), stop=(b == 1))
                last.then_inc(F("up_done"), 1)

            def transpose_weights(c):
                pe.wait_ge(F("csplit_ready"), c + 1)
                for t in range(TILES):
                    last = nc.tensor.transpose(bk_act[0:PARTS, t * 64:(t + 1) * 64].bitcast(bf16),
                                               csplit[:, t, :, :].rearrange("p s e -> p (s e)"), ident16[:, :])
                last.then_inc(F("combt_done"), 1)

            def spread(c, q):
                if q == 0:
                    pe.wait_ge(F("combt_ready"), c + 1)
                if q < 2:
                    pe.wait_ge(F("hids_ready"), c * PAIRS)
                else:
                    pe.wait_ge(F("hids_ready"), c * PAIRS + q - 1)
                nc.tensor.matmul(bk_gate[q % 2][:, :], select16[:, q, :], comb_t[:, :],
                                 start=True, stop=True).then_inc(F("gate_done"), 1)

            def down(c):
                pe.wait_ge(F("hids_ready"), (c + 1) * PAIRS)
                o = [bk_act[m * C:(m + 1) * C, 0:CT // 2] for m in range(2)]
                half = [slice(m * (CT // 2), (m + 1) * (CT // 2)) for m in range(2)]
                for b in range(SPLIT):
                    for m in range(2):
                        nc.tensor.matmul(o[m], b2split[:, b, :], comb_t[:, half[m]], start=(b == 0), stop=False)
                for q in range(PAIRS):
                    for m in range(2):
                        last = nc.tensor.matmul(o[m], w2c[:, q, :], hids[:, q, half[m]],
                                                start=False, stop=(q == PAIRS - 1))
                last.then_inc(F("down_done"), 1)

            def back_to_tokens(c, par):
                pe.wait_ge(F("y2t_ready"), c + 1)
                pe.wait_ge(F("ot_ready"), c)
                for t in range(TILES):
                    m, u = t // 2, t % 2
                    nc.tensor.matmul(bk_y2[:, t * C:(t + 1) * C], h1_t[par][:, t * 128:(t + 1) * 128],
                                     twice_c[:, :], start=True, stop=False)
                    last = nc.tensor.matmul(bk_y2[:, t * C:(t + 1) * C], y2t[:, u * 128:(u + 1) * 128],
                                            P("ident")[:, m * C:(m + 1) * C], start=False, stop=True)
                last.then_inc(F("back_done"), 1)

            def step(s, it, par, front, middle, back):
                if front:
                    if back:
                        pe.wait_ge(F("y2t_ready"), s - 2)
                    row_products(s, it, par)
                if s == 2:
                    pe.wait_ge(F("s_setup"), 1)
                if back:
                    up(s - 2, 0, par)
                    up(s - 2, 1, par)
                if middle:
                    gram(s - 1)
                if front:
                    transpose_rows(s)
                if back:
                    up(s - 2, 2, par)
                if front:
                    if middle:
                        pe.wait_ge(F("gm_ready"), s)
                    column_products(s)
                if back:
                    up(s - 2, 3, par)
                    if front:
                        pe.wait_ge(F("cols_ready"), s + 1)
                    transpose_weights(s - 2)
                if middle:
                    if front:
                        pe.wait_ge(F("expand_ready"), s + 1)
                    attention(s - 1)
                if back:
                    spread(s - 2, 0)
                    spread(s - 2, 1)
                if front:
                    if back:
                        pe.wait_ge(F("combt_ready"), s - 1)
                    tokens(s)
                if back:
                    spread(s - 2, 2)
                    spread(s - 2, 3)
                if front:
                    head_centred(s)
                if back:
                    down(s - 2)
                if middle:
                    transpose_h1(s - 1)
                if back:
                    back_to_tokens(s - 2, par)
                if middle:
                    router(s - 1, 1 - par)
            steps(pe, step)


def resize_operator(size):
    scale = size / GRID
    at = (np.arange(GRID) + 0.5) * scale - 0.5
    w = np.maximum(0.0, 1.0 - np.abs(at[:, None] - np.arange(size)[None, :]) / scale)
    return w / w.sum(axis=1, keepdims=True)


def axis_operator():
    def haar(size, sign):
        m = np.zeros((size // 2, size))
        m[np.arange(size // 2), np.arange(0, size, 2)] = 0.5 ** 0.5
        m[np.arange(size // 2), np.arange(1, size, 2)] = sign * 0.5 ** 0.5
        return m
    low1, high1 = haar(SIDE, 1), haar(SIDE, -1)
    low2, high2 = haar(SIDE // 2, 1) @ low1, haar(SIDE // 2, -1) @ low1
    r1, r2 = resize_operator(SIDE // 2), resize_operator(SIDE // 4)
    return np.concatenate([r1 @ low1, r1 @ high1, r2 @ low2, r2 @ high2]).astype(np.float32)


def kernel(x, L0_tok_W, L0_tok_b, L0_attn_kln_weight, L0_attn_kln_bias, L0_attn_vln_weight, L0_attn_vln_bias,
           L0_ffn_router_w, L0_ffn_w1, L0_ffn_b1, L0_ffn_w2, L0_ffn_b2):
    import concourse.bacc as bacc
    from concourse.bass_utils import run_bass_kernel_spmd

    x = np.ascontiguousarray(x)
    blocks = [(FIRST_AT, np.zeros((128, FIRST), np.float32)), (MAIN_AT, np.zeros((128, MAIN), np.float32)),
              (PART_AT, np.zeros((PARTS, PART), np.float32))]

    def put(name, value):
        for at, block in blocks:
            if name in at:
                a, b = at[name]
                block[:, a:b] = np.asarray(value).reshape(block.shape[0], b - a)

    op = axis_operator()
    centre = np.eye(C) - 1 / C
    put("rows_op", op.T.reshape(128, 2, OPS))
    put("cols_op", op.T.reshape(2, 128, OPS).transpose(1, 0, 2))
    put("ident", np.eye(128))
    put("jmask", np.tile(np.eye(GRID), (128 // GRID, 1)))
    put("head_centre", np.tile(np.kron(np.eye(HEADS), np.eye(HEAD) - 1 / HEAD), (2, 1)))
    put("headmask", np.tile(np.kron(np.eye(HEADS), np.ones((HEAD, HEAD))) / TOKENS, (2, 1)))
    put("twice", np.tile(2 * np.eye(C), (2, 1)))
    put("twice_centre", np.tile(2 * centre, (2, 1)))
    sel = np.zeros((SPLIT, EXPERTS, PAIRS, 2, FF), np.float32)
    for e in range(EXPERTS):
        sel[:, e, e // 2, e % 2, :] = 0.5
    put("select", sel)
    i, j = np.arange(EXPERTS)[:, None], np.arange(EXPERTS)[None, :]
    put("before", np.broadcast_to(j < i, (128, EXPERTS, EXPERTS)))
    put("rank_limit", np.broadcast_to(np.arange(EXPERTS) - (EXPERTS - 1) + 1.5, (128, TILES, EXPERTS)))
    w = np.zeros((KINDS, KINDS, GRID, C), np.float32)
    for m, (a, b) in enumerate(MAPS):
        w[a, b] = np.broadcast_to(np.asarray(L0_tok_W)[m], (GRID, C))
    put("wtok", w)
    put("btok_col", np.tile(np.asarray(L0_tok_b), 2))
    for name, value in (("kw", L0_attn_kln_weight), ("kb", L0_attn_kln_bias), ("vw", L0_attn_vln_weight),
                        ("vb", L0_attn_vln_bias)):
        put(name, np.broadcast_to(np.asarray(value).reshape(C), (128, C)))
    put("w1", np.tile(np.asarray(L0_ffn_w1).transpose(1, 0, 2).reshape(C, EXPERTS * FF), (2, 1)))
    put("b1", np.asarray(L0_ffn_b1).reshape(PAIRS, 2 * FF).T)
    put("w2", np.asarray(L0_ffn_w2).reshape(PAIRS, 2 * FF, C).transpose(1, 0, 2))
    put("router", np.tile(np.asarray(L0_ffn_router_w).T, (2, 1)))
    put("b2", np.tile(np.asarray(L0_ffn_b2), (SPLIT, 1)))

    nc = bacc.Bacc("TRN2", target_bir_lowering=False, num_devices=1)
    arrays = {"x_dram": x, "first_dram": blocks[0][1], "main_dram": blocks[1][1], "part_dram": blocks[2][1]}
    args = [nc.dram_tensor(name, a.shape, mybir.dt.float32, kind="ExternalInput").ap() for name, a in arrays.items()]
    out = nc.dram_tensor("out_dram", (IMAGES, TOKENS, C), mybir.dt.float32, kind="ExternalOutput").ap()
    vit_tower_kernel(nc, *args, out)
    r = run_bass_kernel_spmd(nc, [arrays], core_ids=[0])
    return r.results[0]["out_dram"]
```

```python
from contextlib import ExitStack

import numpy as np

import concourse.bass as bass
from concourse import mybir

IMAGES, SIDE = 64, 256
GRID = 8
TOKENS = GRID * GRID
C = 64
HEADS = 8
HEAD = C // HEADS
EXPERTS = 8
FF = 64
KINDS = 4
OPS = KINDS * GRID

CHUNK = 8
CHUNKS = IMAGES // CHUNK
TILES = CHUNK * TOKENS // 128
CT = CHUNK * TOKENS
GROUPS = CHUNK // 2
PAIRS = EXPERTS // 2
SPLIT = 3
LAG = 8
STEPS = CHUNKS + LAG
NEWTON = 3
RSQRT_MAGIC = 0x5F3759DF

LOW1, HIGH1, LOW2, HIGH2 = range(KINDS)
MAPS = [(LOW2, LOW2), (HIGH2, LOW2), (LOW2, HIGH2), (HIGH2, HIGH2),
        (HIGH1, LOW1), (LOW1, HIGH1), (HIGH1, HIGH1)]


def layout(fields):
    at, end = {}, 0
    for name, width in fields:
        at[name] = (end, end + width)
        end += width
    return at, end


FIRST_AT, FIRST = layout([("rows_op", 2 * OPS), ("cols_op", 2 * OPS), ("ident", 128), ("jmask", GRID), ("wtok", C),
                          ("btok_col", 1), ("head_centre", C)])
SECOND_AT, SECOND = layout([("kw", C), ("kb", C), ("vw", C), ("vb", C), ("headmask", C), ("twice", C)])
MAIN_AT, MAIN = layout([
    ("w1", PAIRS * 128), ("router", EXPERTS), ("twice_centre", 2 * 128),
    ("b1", PAIRS), ("w2", PAIRS * C), ("before", EXPERTS * EXPERTS), ("rank_limit", TILES * EXPERTS)])
PART_AT, PART = layout([("b2", C), ("select", PAIRS * 128)])
PARTS = SPLIT * 4 * EXPERTS


def vit_tower_kernel(nc, x, first, second, main, part, out):
    fp32, bf16, fp32r, i32 = mybir.dt.float32, mybir.dt.bfloat16, mybir.dt.float32r, mybir.dt.int32
    ALU, ACT, AX = mybir.AluOpType, mybir.ActivationFunctionType, mybir.AxisListType

    x_v = x.rearrange("(c n) one (p s) w -> c p n (one s w)", n=CHUNK, s=2)
    out_v = out.rearrange("(c t two) k w -> c (two k) t w", t=TILES, two=2)

    with ExitStack() as ctx:
        def sb(name, shape, dt=fp32):
            return ctx.enter_context(nc.sbuf_tensor(name, shape, dt))

        def ps(name):
            return ctx.enter_context(nc.psum_tensor(name, [128, 512], fp32))

        def sem(name):
            return ctx.enter_context(nc.semaphore(name))

        first_sb = sb("first_sb", [128, FIRST])
        second_sb = sb("second_sb", [128, SECOND])
        main_sb = sb("main_sb", [128, MAIN])
        part_sb = sb("part_sb", [PARTS, PART])

        def P(name):
            for tile, at in ((first_sb, FIRST_AT), (second_sb, SECOND_AT), (main_sb, MAIN_AT), (part_sb, PART_AT)):
                if name in at:
                    return tile[:, at[name][0]:at[name][1]]

        def over(ap, count):
            return ap.unsqueeze(len(ap.shape)).to_broadcast([*ap.shape, count])

        def per_tile(name):
            return P(name).unsqueeze(1).to_broadcast([128, TILES, C])

        small, groups = [128, TILES, EXPERTS], [128, TILES * HEADS]
        xt = [sb(f"xt{i}", [128, CHUNK, 2, SIDE]) for i in range(2)]
        rows = sb("rows", [128, 512])
        cols = sb("cols", [128, 2, 2, GROUPS, KINDS, GRID])
        expand = sb("expand", [128, CHUNK, GRID, GRID])
        h_t = [sb(f"h_t{i}", [128, TILES, TOKENS]) for i in range(2)]
        dsq = sb("dsq", [128, TILES, C])
        dvar, dstd, dste, drec = (sb(f"d_{x}", groups) for x in ("var", "std", "ste", "rec"))
        dnewton = [sb(f"d_newton{i}", groups) for i in range(NEWTON)]
        dtmp = [sb(f"d_tmp{i}", groups) for i in range(2)]
        n, k0, v0, k, v = (sb(x, [128, TILES, C]) for x in ("n", "k0", "v0", "k", "v"))
        gm, kv = sb("gm", [128, TILES, C]), sb("kv", [128, TILES, C])
        yc, ysq = sb("yc", [128, TILES, C]), sb("ysq", [128, TILES, C])
        ysum, yss, yvar, yrstd = (sb(f"y_{x}", [128, TILES]) for x in ("sum", "ss", "var", "rstd"))
        h1 = sb("h1", [128, TILES, C])
        h1s = sb("h1s", [128, TILES, 2, C], fp32r)
        h1_t = [sb(f"h1_t{i}", [128, CT], fp32r) for i in range(2)]
        lmax = sb("lmax", [128, TILES])
        logits, lsh, ztop, arg, th = (sb(x, small) for x in ("logits", "lsh", "ztop", "arg", "th"))
        ge, geb, gd = (sb(x, [128, TILES, EXPERTS, EXPERTS]) for x in ("ge", "geb", "gd"))
        rank, top, comb, crest, crest2 = (sb(x, small) for x in ("rank", "top", "comb", "crest", "crest2"))
        zsum = sb("zsum", [128, TILES])
        csplit = sb("csplit", [128, TILES, SPLIT, 4, EXPERTS], bf16)
        comb_t = sb("comb_t", [PARTS, CT], bf16)
        hid = sb("hid", [128, PAIRS, CT])
        hids = sb("hids", [128, PAIRS, CT])
        y2t = sb("y2t", [128, CT // 2])
        y2sq = sb("y2sq", [128, TILES, C])
        y2ss, y2var, y2rstd = (sb(f"y2_{x}", [128, TILES]) for x in ("ss", "var", "rstd"))
        ot = [sb(f"ot{i}", [128, TILES, C]) for i in range(2)]

        table_out = sb("table_out", [128, 1])
        neghalf = sb("neghalf", [128, TILES])
        ident16 = sb("ident16", [128, 128], bf16)
        select16 = sb("select16", [PARTS, PAIRS, 128], bf16)
        b2sum, b2half, b2c = sb("b2sum", [PARTS, 1]), sb("b2half", [PARTS, C]), sb("b2c", [PARTS, C])
        b2split = sb("b2split", [PARTS, SPLIT, C], bf16)
        b2rest = sb("b2rest", [PARTS, 2, C])
        b2stack = sb("b2stack", [PARTS, C], bf16)
        w1s = sb("w1s", [128, 2, PAIRS, 128], fp32r)
        routers = sb("routers", [128, 2 * EXPERTS], fp32r)
        twice_c = sb("twice_c", [128, 2, 128], fp32r)
        w2sum, w2c = sb("w2sum", [128, PAIRS]), sb("w2c", [128, PAIRS, C])

        bk = {}
        bk.update(dict.fromkeys(["down"], ps("bank0")))
        bk.update(dict.fromkeys(["tok", "h1t", "router"], ps("bank1")))
        bk.update(dict.fromkeys(["gram", "up2", "combt", "gate0"], ps("bank2")))
        bk.update(dict.fromkeys(["q", "gate1", "gate3"], ps("bank3")))
        bk.update(dict.fromkeys(["rows", "y2"], ps("bank4")))
        bk.update(dict.fromkeys(["cols", "up0", "gate2"], ps("bank5")))
        bk.update(dict.fromkeys(["y", "up1", "up3"], ps("bank6")))
        bk.update(dict.fromkeys(["d"], ps("bank7")))

        sems = {}

        def F(name):
            if name not in sems:
                sems[name] = sem(name)
            return sems[name]

        x_loaded = [[sem(f"x_loaded{i}{j}") for j in range(2)] for i in range(2)]
        x_first_loaded = [sem(f"x_first_loaded{g}") for g in range(GROUPS)]
        stored = [sem(f"stored{i}") for i in range(2)]

        def held(chunk):
            return min(max(chunk + 1, 0), CHUNKS)

        def on(chunk, stage, *args):
            if 0 <= chunk < CHUNKS:
                stage(chunk, *args)

        def tiles_of(bank):
            return bank[:, 0:TILES * C].rearrange("p (t e) -> p t e", e=C)

        block = ctx.enter_context(nc.Block())

        @block.sync
        def _(sp):
            def load(c):
                if c >= 2:
                    sp.wait_ge(F("s1_done"), c - 1)
                for h in range(2):
                    sp.dma_start(xt[c % 2][:, h * 4:h * 4 + 4, :, :],
                                 x_v[c, :, h * 4:h * 4 + 4, :].rearrange("p n (s w) -> p n s w", s=2)
                                 ).then_inc(x_loaded[c % 2][h], 16)

            def store(c):
                sp.wait_ge(F("ot_ready"), c + 1)
                sp.dma_start(out_v[c, :, :, :], ot[c % 2][:, :, :]).then_inc(stored[c % 2], 16)

            sp.dma_start(first_sb[:, :], first).then_inc(F("s_first"), 16)
            for g in range(GROUPS):
                sp.dma_start(xt[0][:, 2 * g:2 * g + 2, :, :],
                             x_v[0, :, 2 * g:2 * g + 2, :].rearrange("p n (s w) -> p n s w", s=2)
                             ).then_inc(x_first_loaded[g], 16)
            sp.dma_start(second_sb[:, :], second).then_inc(F("s_second"), 16)
            load(1)
            sp.dma_start(main_sb[:, :], main).then_inc(F("s_main"), 16)
            sp.dma_start(part_sb[:, :], part).then_inc(F("s_part"), 16)
            for s in range(STEPS):
                on(s + 2, load)
                on(s - LAG, store)
            for par in range(2):
                sp.wait_ge(stored[par], 16 * (CHUNKS // 2))

        @block.gpsimd
        def _(pool):
            tt, ts = nc.gpsimd.tensor_tensor, nc.gpsimd.tensor_scalar
            nc.gpsimd.memset(csplit[:, :, :, :, :], 0.0)
            nc.gpsimd.memset(neghalf[:, :], -0.5).then_inc(F("s_consts"), 1)
            pool.wait_ge(F("s_consts"), 1)
            pool.wait_ge(F("s_main"), 16)
            pool.wait_ge(F("s_w1"), 1)
            tt(w1s[:, 1, :, :].rearrange("p q m -> p (q m)"), P("w1"),
               w1s[:, 0, :, :].rearrange("p q m -> p (q m)").bitcast(fp32), ALU.subtract).then_inc(F("s_pool_setup"), 1)
            pool.wait_ge(F("s_second"), 16)

            def kv_matrix(c):
                pool.wait_ge(F("gm_ready"), c + 1)
                pool.wait_ge(F("y_done"), c)
                tt(kv[:, :, :], gm[:, :, :], per_tile("twice"), ALU.add).then_inc(F("kv_ready"), 1)

            def variance(c, ss, var, ready, done):
                pool.wait_ge(F(ready), c + 1)
                ts(var[:, :], ss[:, :], 1.0 / C, 1e-5, ALU.mult, ALU.add).then_inc(F(done), 1)

            def rstd(c, var, out_, ready, used, done):
                pool.wait_ge(F(ready), c + 1)
                pool.wait_ge(F(used), c)
                tt(out_[:, :], var[:, :], neghalf[:, :], ALU.pow).then_inc(F(done), 1)

            def keys0(c):
                pool.wait_ge(F("n_ready"), c + 1)
                tt(k0[:, :, :], n[:, :, :], per_tile("kw"), ALU.mult).then_inc(F("k0_ready"), 1)

            def values0(c):
                pool.wait_ge(F("n_ready"), c + 1)
                tt(v0[:, :, :], n[:, :, :], per_tile("vw"), ALU.mult).then_inc(F("v0_ready"), 1)

            def keys(c):
                pool.wait_ge(F("k0_ready"), c + 1)
                pool.wait_ge(F("g_done"), c)
                tt(k[:, :, :], k0[:, :, :], per_tile("kb"), ALU.add).then_inc(F("k_ready"), 1)

            def values(c):
                pool.wait_ge(F("v0_ready"), c + 1)
                pool.wait_ge(F("g_done"), c)
                tt(v[:, :, :], v0[:, :, :], per_tile("vb"), ALU.add).then_inc(F("v_ready"), 1)

            def ranks_before(c):
                pool.wait_ge(F("ge_ready"), c + 1)
                tt(geb[:, :, :, :].rearrange("p t i j -> p t (i j)"), ge[:, :, :, :].rearrange("p t i j -> p t (i j)"),
                   P("before").unsqueeze(1).to_broadcast([128, TILES, EXPERTS * EXPERTS]), ALU.mult
                   ).then_inc(F("geb_ready"), 1)

            def ranks_antisymmetric(c):
                pool.wait_ge(F("geb_ready"), c + 1)
                pool.wait_ge(F("rank_ready"), c)
                tt(gd[:, :, :, :], geb[:, :, :, :], geb[:, :, :, :].rearrange("p t i j -> p t j i"), ALU.subtract
                   ).then_inc(F("gd_ready"), 1)

            def copies(x):
                return x[:, :, :].unsqueeze(2).to_broadcast([128, TILES, SPLIT, EXPERTS])

            def split_first(c):
                pool.wait_ge(F("comb_ready"), c + 1)
                pool.wait_ge(F("combt_done"), c)
                nc.gpsimd.tensor_copy(csplit[:, :, :, 0, :], copies(comb)).then_inc(F("chi_ready"), 1)

            def split_rest(c):
                pool.wait_ge(F("chi_ready"), c + 1)
                tt(crest[:, :, :], comb[:, :, :], csplit[:, :, 0, 0, :], ALU.subtract).then_inc(F("crest_ready"), 1)

            def split_second(c):
                pool.wait_ge(F("crest_ready"), c + 1)
                nc.gpsimd.tensor_copy(csplit[:, :, :, 1, :], copies(crest)).then_inc(F("cmid_ready"), 1)

            def split_rest2(c):
                pool.wait_ge(F("cmid_ready"), c + 1)
                tt(crest2[:, :, :], crest[:, :, :], csplit[:, :, 0, 1, :], ALU.subtract).then_inc(F("crest2_ready"), 1)

            def split_third(c):
                pool.wait_ge(F("crest2_ready"), c + 1)
                nc.gpsimd.tensor_copy(csplit[:, :, :, 2, :], copies(crest2)).then_inc(F("csplit_ready"), 1)

            for s in range(STEPS):
                on(s - 3, keys)
                on(s - 3, values)
                on(s - 6, split_first)
                on(s - 4, variance, yss, yvar, "yss_ready", "yvar_ready")
                on(s - 6, split_rest)
                on(s - 4, rstd, yvar, yrstd, "yvar_ready", "h1_ready", "yrstd_ready")
                on(s - 6, split_second)
                on(s - 3, kv_matrix)
                on(s - 6, split_rest2)
                on(s - 6, split_third)
                on(s - 5, ranks_before)
                on(s - 8, variance, y2ss, y2var, "y2ss_ready", "y2var_ready")
                on(s - 5, ranks_antisymmetric)
                on(s - 8, rstd, y2var, y2rstd, "y2var_ready", "ot_ready", "y2rstd_ready")
                on(s - 2, keys0)
                on(s - 2, values0)

        @block.scalar
        def _(act):
            act.wait_ge(F("s_first"), 16)
            nc.scalar.activation(table_out[:, :], P("ident")[:, 0:1], ACT.Gelu)

            def setup():
                act.wait_ge(F("s_main"), 16)
                nc.scalar.activation(w1s[:, 0, :, :].rearrange("p q m -> p (q m)"), P("w1"), ACT.Copy
                                     ).then_inc(F("s_w1"), 1)
                nc.scalar.activation(twice_c[:, :, :].rearrange("p m e -> p (m e)"), P("twice_centre"), ACT.Copy)
                act.wait_ge(F("s_part"), 16)
                nc.scalar.activation(select16[:, :, :].rearrange("p q m -> p (q m)"), P("select"), ACT.Copy
                                     ).then_inc(F("s_act_setup"), 1)

            def rows_copy(c):
                act.wait_ge(F("s1_done"), c + 1)
                act.wait_ge(F("t_done"), c)
                nc.scalar.activation(rows[:, :], bk["rows"][:, :], ACT.Copy).then_inc(F("rows_ready"), 1)

            def cols_copy(c):
                act.wait_ge(F("t_done"), c + 1)
                act.wait_ge(F("q_done"), c)
                nc.scalar.activation(cols[:, :, :, :, :, :].rearrange("p a b g t i -> p (a b g t i)"),
                                     bk["cols"][:, :], ACT.Copy).then_inc(F("cols_ready"), 1)

            def square(c, out_, in_, ready, used, done, scale=1.0):
                act.wait_ge(F(ready), c + 1)
                act.wait_ge(F(used), c)
                nc.scalar.activation(out_[:, :, :], in_, ACT.Square, scale=scale).then_inc(F(done), 1)

            def gelu(c, q):
                if c == 0:
                    act.wait_ge(F("s_main"), 16)
                act.wait_ge(F(f"up{q}_done"), c + 1)
                act.wait_ge(F(f"hids{q}_ready"), c)
                nc.scalar.activation(hid[:, q, :], bk[f"up{q}"][:, :], ACT.Gelu,
                                     bias=P("b1")[:, q:q + 1]).then_inc(F(f"hid{q}_ready"), 1)

            def h1_upper(c):
                act.wait_ge(F("h1_ready"), c + 1)
                act.wait_ge(F("h1t_done"), c)
                nc.scalar.activation(h1s[:, :, 0, :], h1[:, :, :], ACT.Copy).then_inc(F("h1_upper"), 1)

            def h1t_copy(c):
                act.wait_ge(F("h1t_done"), c + 1)
                if c >= 2:
                    act.wait_ge(F("biases_done"), c - 1)
                nc.scalar.activation(h1_t[c % 2][:, :], bk["h1t"][:, :], ACT.Copy).then_inc(F("h1t_ready"), 1)

            def combt_copy(c):
                act.wait_ge(F("combt_done"), c + 1)
                act.wait_ge(F("gate3_done"), c)
                nc.scalar.activation(comb_t[:, :], bk["combt"][0:PARTS, 0:CT // 2].bitcast(bf16),
                                     ACT.Copy).then_inc(F("combt_ready"), 1)

            def ht_copy(c):
                act.wait_ge(F("ht_done"), c + 1)
                if c >= 2:
                    act.wait_ge(F("y_done"), c - 1)
                nc.scalar.activation(h_t[c % 2][:, :, :].rearrange("p t k -> p (t k)"), bk["tok"][:, 0:TILES * TOKENS],
                                     ACT.Identity, bias=P("btok_col")).then_inc(F("ht_ready"), 1)

            def tanh(c):
                act.wait_ge(F("arg_ready"), c + 1)
                act.wait_ge(F("comb_ready"), c)
                nc.scalar.activation(th[:, :, :], arg[:, :, :], ACT.Tanh).then_inc(F("th_ready"), 1)

            def y2t_copy(c):
                act.wait_ge(F("down3_done"), c + 1)
                act.wait_ge(F("back_done"), c)
                nc.scalar.activation(y2t[:, :], bk["down"][:, 0:CT // 2], ACT.Copy).then_inc(F("y2t_ready"), 1)

            for s in range(STEPS):
                on(s - 7, gelu, 3)
                on(s - 6, tanh)
                on(s - 5, h1t_copy)
                on(s, rows_copy)
                on(s - 8, square, y2sq, tiles_of(bk["y2"]), "back_done", "y2ss_ready", "y2sq_ready")
                on(s - 6, gelu, 1)
                on(s, cols_copy)
                if s == 1:
                    setup()
                on(s - 6, gelu, 2)
                on(s - 4, h1_upper)
                on(s - 1, ht_copy)
                on(s - 6, combt_copy)
                on(s - 3, square, ysq, yc[:, :, :], "yc_ready", "yss_ready", "ysq_ready")
                on(s - 1, square, dsq, tiles_of(bk["d"]), "d_done", "dvar_ready", "dsq_ready", (HEAD - 1) ** -0.5)
                on(s - 6, gelu, 0)
                on(s - 7, y2t_copy)

        @block.vector
        def _(dve):
            tt, stt, ts = nc.vector.tensor_tensor, nc.vector.scalar_tensor_tensor, nc.vector.tensor_scalar
            rsum, copy = nc.vector.reduce_sum, nc.vector.tensor_copy
            dve.wait_ge(F("s_first"), 16)
            copy(ident16[:, :], P("ident"))
            def setup():
                dve.wait_ge(F("s_main"), 16)
                copy(routers[:, 0:EXPERTS], P("router")).then_inc(F("s_router"), 1)
                w2 = P("w2").rearrange("p (q e) -> p q e", e=C)
                rsum(w2sum[:, :], w2, AX.X).then_inc(F("s_w2"), 1)
                dve.wait_ge(F("s_part"), 16)
                rsum(b2sum[:, :], P("b2"), AX.X)
                ts(b2half[:, :], P("b2"), 0.5, None, ALU.mult).then_inc(F("s_b2"), 1)
                dve.wait_ge(F("s_router"), 1)
                tt(routers[:, EXPERTS:], P("router"), routers[:, 0:EXPERTS].bitcast(fp32), ALU.subtract)
                dve.wait_ge(F("s_w2"), 1)
                stt(w2c[:, :, :], over(w2sum[:, :], C), -1.0 / C, w2, ALU.mult, ALU.add)
                dve.wait_ge(F("s_b2"), 1)
                stt(b2c[:, :], b2sum[:, :].to_broadcast([PARTS, C]), -0.5 / C, b2half[:, :], ALU.mult, ALU.add
                    ).then_inc(F("s_b2c"), 1)
                dve.wait_ge(F("s_b2c"), 1)
                copy(b2split[:, 0, :], b2c[:, :]).then_inc(F("s_b2d"), 1)
                dve.wait_ge(F("s_b2d"), 1)
                tt(b2rest[:, 0, :], b2c[:, :], b2split[:, 0, :], ALU.subtract).then_inc(F("s_b2e"), 1)
                dve.wait_ge(F("s_b2e"), 1)
                copy(b2split[:, 1, :], b2rest[:, 0, :]).then_inc(F("s_b2f"), 1)
                dve.wait_ge(F("s_b2f"), 1)
                tt(b2rest[:, 1, :], b2rest[:, 0, :], b2split[:, 1, :], ALU.subtract).then_inc(F("s_b2g"), 1)
                dve.wait_ge(F("s_b2g"), 1)
                copy(b2split[:, 2, :], b2rest[:, 1, :]).then_inc(F("s_b2h"), 1)
                dve.wait_ge(F("s_b2h"), 1)
                for r in range(SPLIT):
                    o = slice(r * 4 * EXPERTS, (r + 1) * 4 * EXPERTS)
                    last = copy(b2stack[o, :], b2split[o, r, :])
                last.then_inc(F("s_setup"), 1)

            def mask_gram(c):
                if c == 0:
                    dve.wait_ge(F("s_second"), 16)
                dve.wait_ge(F("g_done"), c + 1)
                dve.wait_ge(F("kv_ready"), c)
                tt(gm[:, :, :], tiles_of(bk["gram"]), per_tile("headmask"), ALU.mult).then_inc(F("gm_ready"), 1)

            def norm1_mean(c):
                dve.wait_ge(F("y_done"), c + 1)
                rsum(ysum[:, :], tiles_of(bk["y"]), AX.X).then_inc(F("ysum_ready"), 1)

            def norm1_centre(c):
                dve.wait_ge(F("ysum_ready"), c + 1)
                stt(yc[:, :, :], over(ysum[:, :], C), -1.0 / C, tiles_of(bk["y"]), ALU.mult, ALU.add
                    ).then_inc(F("yc_ready"), 1)

            def norm1_sum(c):
                dve.wait_ge(F("ysq_ready"), c + 1)
                dve.wait_ge(F("yvar_ready"), c)
                rsum(yss[:, :], ysq[:, :, :], AX.X).then_inc(F("yss_ready"), 1)

            def norm1_scale(c):
                dve.wait_ge(F("yrstd_ready"), c + 1)
                tt(h1[:, :, :], yc[:, :, :], over(yrstd[:, :], C), ALU.mult).then_inc(F("h1_ready"), 1)

            def h1_lower(c):
                dve.wait_ge(F("h1_upper"), c + 1)
                dve.wait_ge(F("h1t_done"), c)
                tt(h1s[:, :, 1, :], h1[:, :, :], h1s[:, :, 0, :].bitcast(fp32), ALU.subtract
                   ).then_inc(F("h1_lower"), 1)

            def expand_columns(c):
                dve.wait_ge(F("q_done"), c + 1)
                dve.wait_ge(F("ht_done"), c)
                tt(expand[:, :, :, :].rearrange("p n i j -> p (n i) j"), over(bk["q"][:, 0:CHUNK * GRID], GRID),
                   P("jmask").unsqueeze(1).to_broadcast([128, CHUNK * GRID, GRID]), ALU.mult
                   ).then_inc(F("expand_ready"), 1)

            def logits_sum(c):
                both = bk["router"][:, 0:TILES * 2 * EXPERTS].rearrange("p (t b e) -> p t b e", b=2, e=EXPERTS)
                dve.wait_ge(F("logits_done"), c + 1)
                rsum(logits[:, :, :], both.rearrange("p t b e -> p t e b"), AX.X).then_inc(F("logits_ready"), 1)

            def logits_max(c):
                dve.wait_ge(F("logits_ready"), c + 1)
                nc.vector.reduce_max(lmax[:, :], logits[:, :, :], AX.X).then_inc(F("lmax_ready"), 1)

            def logits_shift(c):
                dve.wait_ge(F("lmax_ready"), c + 1)
                tt(lsh[:, :, :], logits[:, :, :], over(lmax[:, :], EXPERTS), ALU.subtract
                   ).then_inc(F("lsh_ready"), 1)

            def logits_compare(c):
                dve.wait_ge(F("lsh_ready"), c + 1)
                dve.wait_ge(F("geb_ready"), c)
                tt(ge[:, :, :, :], lsh[:, :, :].unsqueeze(2).to_broadcast([128, TILES, EXPERTS, EXPERTS]),
                   over(lsh[:, :, :], EXPERTS), ALU.is_ge).then_inc(F("ge_ready"), 1)

            def rank_sum(c):
                dve.wait_ge(F("gd_ready"), c + 1)
                rsum(rank[:, :, :], gd[:, :, :, :], AX.X).then_inc(F("rank_ready"), 1)

            def rank_top2(c):
                dve.wait_ge(F("rank_ready"), c + 1)
                tt(top[:, :, :], rank[:, :, :], P("rank_limit").rearrange("p (t e) -> p t e", e=EXPERTS), ALU.is_le
                   ).then_inc(F("top_ready"), 1)

            def top2_logits(c):
                dve.wait_ge(F("top_ready"), c + 1)
                tt(ztop[:, :, :], lsh[:, :, :], top[:, :, :], ALU.mult).then_inc(F("ztop_ready"), 1)

            def top2_sum(c):
                dve.wait_ge(F("ztop_ready"), c + 1)
                rsum(zsum[:, :], ztop[:, :, :], AX.X).then_inc(F("zsum_ready"), 1)

            def weight_argument(c):
                dve.wait_ge(F("zsum_ready"), c + 1)
                dve.wait_ge(F("th_ready"), c)
                stt(arg[:, :, :], over(zsum[:, :], EXPERTS), -0.5, lsh[:, :, :], ALU.mult, ALU.add
                    ).then_inc(F("arg_ready"), 1)

            def weights(c):
                dve.wait_ge(F("th_ready"), c + 1)
                dve.wait_ge(F("crest_ready"), c)
                stt(comb[:, :, :], th[:, :, :], 1.0, top[:, :, :], ALU.add, ALU.mult).then_inc(F("comb_ready"), 1)

            def gate(c, q):
                dve.wait_ge(F(f"gate{q}_done"), c + 1)
                dve.wait_ge(F(f"hid{q}_ready"), c + 1)
                dve.wait_ge(F(f"down{q}_done"), c)
                tt(hids[:, q, :], hid[:, q, :], bk[f"gate{q}"][:, :], ALU.mult).then_inc(F(f"hids{q}_ready"), 1)

            def head_variance(c):
                dve.wait_ge(F("dsq_ready"), c + 1)
                rsum(dvar[:, :], dsq[:, :, :].rearrange("p t (g e) -> p (t g) e", e=HEAD), AX.X
                     ).then_inc(F("dvar_ready"), 1)

            def head_guess(c):
                dve.wait_ge(F("dvar_ready"), c + 1)
                ts(dnewton[0][:, :].bitcast(i32), dvar[:, :].bitcast(i32), -0.5, float(RSQRT_MAGIC), ALU.mult, ALU.add
                   ).then_inc(F("dnewton0_ready"), 1)

            def newton_first(c, i):
                dve.wait_ge(F(f"dnewton{i}_ready"), c + 1)
                tt(dtmp[0][:, :], dvar[:, :], dnewton[i][:, :], ALU.mult).then_inc(F(f"dn_a{i}"), 1)

            def newton_second(c, i):
                dve.wait_ge(F(f"dn_a{i}"), c + 1)
                stt(dtmp[1][:, :], dtmp[0][:, :], -0.5, dnewton[i][:, :], ALU.mult, ALU.mult
                    ).then_inc(F(f"dn_b{i}"), 1)

            def newton_third(c, i):
                dve.wait_ge(F(f"dn_b{i}"), c + 1)
                if i + 1 < NEWTON:
                    stt(dnewton[i + 1][:, :], dtmp[1][:, :], 1.5, dnewton[i][:, :], ALU.add, ALU.mult
                        ).then_inc(F(f"dnewton{i + 1}_ready"), 1)
                else:
                    stt(dstd[:, :], dtmp[1][:, :], 1.5, dtmp[0][:, :], ALU.add, ALU.mult
                        ).then_inc(F("dstd_ready"), 1)

            def head_eps(c):
                dve.wait_ge(F("dstd_ready"), c + 1)
                ts(dste[:, :], dstd[:, :], 1e-5, None, ALU.add).then_inc(F("dste_ready"), 1)

            def head_reciprocal(c):
                dve.wait_ge(F("dste_ready"), c + 1)
                nc.vector.reciprocal(drec[:, :], dste[:, :]).then_inc(F("drec_ready"), 1)

            def head_scale(c):
                dve.wait_ge(F("drec_ready"), c + 1)
                dve.wait_ge(F("k0_ready"), c)
                dve.wait_ge(F("v0_ready"), c)
                tt(n[:, :, :].rearrange("p t (g e) -> p (t g) e", e=HEAD),
                   bk["d"][:, 0:TILES * C].rearrange("p (g e) -> p g e", e=HEAD),
                   over(drec[:, :], HEAD), ALU.mult).then_inc(F("n_ready"), 1)

            def norm2_sum(c):
                dve.wait_ge(F("y2sq_ready"), c + 1)
                dve.wait_ge(F("y2var_ready"), c)
                rsum(y2ss[:, :], y2sq[:, :, :], AX.X).then_inc(F("y2ss_ready"), 1)

            def norm2_scale(c):
                dve.wait_ge(F("y2rstd_ready"), c + 1)
                if c >= 2:
                    dve.wait_ge(stored[c % 2], 16 * (c // 2))
                tt(ot[c % 2][:, :, :], tiles_of(bk["y2"]), over(y2rstd[:, :], C), ALU.mult).then_inc(F("ot_ready"), 1)

            for s in range(STEPS):
                on(s - 6, weight_argument)
                on(s - 2, newton_first, 0)
                on(s - 7, gate, 0)
                on(s - 2, newton_second, 0)
                on(s - 6, weights)
                on(s - 2, newton_third, 0)
                on(s - 2, newton_first, 1)
                on(s - 7, gate, 1)
                on(s - 2, newton_second, 1)
                on(s - 7, gate, 2)
                on(s - 2, newton_third, 1)
                on(s - 3, mask_gram)
                on(s - 2, newton_first, 2)
                on(s - 5, logits_sum)
                on(s - 2, newton_second, 2)
                on(s - 5, logits_max)
                on(s - 2, newton_third, 2)
                on(s - 5, logits_shift)
                on(s - 2, head_eps)
                on(s - 5, logits_compare)
                on(s - 4, norm1_scale)
                on(s - 8, norm2_sum)
                on(s - 2, head_reciprocal)
                on(s - 7, gate, 3)
                on(s - 2, head_scale)
                on(s - 3, norm1_mean)
                on(s - 4, h1_lower)
                on(s - 3, norm1_centre)
                on(s - 5, rank_sum)
                on(s, expand_columns)
                if s == 1:
                    setup()
                on(s - 5, rank_top2)
                on(s - 3, norm1_sum)
                on(s - 5, top2_logits)
                on(s - 1, head_variance)
                on(s - 5, top2_sum)
                on(s - 8, norm2_scale)
                on(s - 1, head_guess)

        @block.tensor
        def _(pe):
            pe.wait_ge(F("s_first"), 16)
            rows_op = P("rows_op").rearrange("p (s m) -> p s m", s=2)
            cols_op = P("cols_op").rearrange("p (s m) -> p s m", s=2)

            def row_products(c, r):
                if r == 0:
                    for h in range(2):
                        pe.wait_ge(x_loaded[c % 2][h], ((c + 1) // 2) * 16)
                for g in range(GROUPS):
                    last = row_product(c, r, g)
                if r == 1:
                    last.then_inc(F("s1_done"), 1)

            def row_product(c, r, g):
                return nc.tensor.matmul(bk["rows"][g * OPS:(g + 1) * OPS, :].rearrange("p (n w) -> p n w", n=2),
                                        rows_op[:, r, :], xt[c % 2][:, 2 * g:2 * g + 2, r, :],
                                        start=(r == 0), stop=(r == 1))

            def keep_clock():
                for i in range(2):
                    nc.tensor.matmul(bk["down"][0:OPS, 0:128], rows_op[:, 0, :], P("ident"), start=True, stop=True)

            for g in range(GROUPS):
                pe.wait_ge(x_first_loaded[g], 16)
                for r in range(2):
                    last = row_product(0, r, g)
            last.then_inc(F("s1_done"), 1)
            keep_clock()

            def transpose_rows(c):
                pe.wait_ge(F("rows_ready"), c + 1)
                for b in range(4):
                    last = nc.tensor.transpose(bk["cols"][:, b * 128:(b + 1) * 128], rows[:, b * 128:(b + 1) * 128],
                                               P("ident"))
                last.then_inc(F("t_done"), 1)

            def column_products(c):
                pe.wait_ge(F("cols_ready"), c + 1)
                for h in range(2):
                    for t in range(KINDS):
                        last = nc.tensor.matmul(bk["q"][t * OPS:(t + 1) * OPS, 0:CHUNK * GRID]
                                                .rearrange("p (g n i) -> p g n i", g=GROUPS, n=2),
                                                cols_op[:, h, :],
                                                cols[:, :, h, :, t, :].rearrange("p n g i -> p g n i"),
                                                start=(h == 0), stop=(h == 1))
                last.then_inc(F("q_done"), 1)

            def tokens(c):
                pe.wait_ge(F("expand_ready"), c + 1)
                ex_v = expand[:, :, :, :].rearrange("p (t n) i j -> p n t (i j)", n=2)
                for m in range(2):
                    last = nc.tensor.matmul(bk["tok"][m * C:(m + 1) * C, 0:TILES * TOKENS]
                                            .rearrange("p (t k) -> p t k", t=TILES),
                                            P("wtok"), ex_v[:, m, :, :], start=True, stop=True)
                last.then_inc(F("ht_done"), 1)

            def by_image(bank, lhs, rhs, done):
                for t in range(TILES):
                    for m in range(2):
                        o = slice(m * 64, m * 64 + 64)
                        last = nc.tensor.matmul(bank[o, t * C:(t + 1) * C], lhs(o, t), rhs(o, t), start=True, stop=True)
                last.then_inc(F(done), 1)

            def head_centred(c):
                pe.wait_ge(F("ht_ready"), c + 1)
                by_image(bk["d"], lambda o, t: h_t[c % 2][o, t, :], lambda o, t: P("head_centre")[o, :], "d_done")

            def gram(c):
                pe.wait_ge(F("k_ready"), c + 1)
                pe.wait_ge(F("v_ready"), c + 1)
                by_image(bk["gram"], lambda o, t: k[o, t, :], lambda o, t: v[o, t, :], "g_done")

            def attention(c):
                pe.wait_ge(F("kv_ready"), c + 1)
                by_image(bk["y"], lambda o, t: h_t[c % 2][o, t, :], lambda o, t: kv[o, t, :], "y_done")

            def transpose_h1(c):
                pe.wait_ge(F("h1_lower"), c + 1)
                for t in range(TILES):
                    last = nc.tensor.transpose(bk["h1t"][:, t * 128:(t + 1) * 128],
                                               h1s[:, t, :, :].rearrange("p r e -> p (r e)").bitcast(fp32), P("ident"))
                last.then_inc(F("h1t_done"), 1)

            def router(c):
                if c == 0:
                    pe.wait_ge(F("s_setup"), 1)
                    pe.wait_ge(F("s_pool_setup"), 1)
                    pe.wait_ge(F("s_act_setup"), 1)
                pe.wait_ge(F("h1t_ready"), c + 1)
                for t in range(TILES):
                    last = nc.tensor.matmul(bk["router"][:, t * 2 * EXPERTS:(t + 1) * 2 * EXPERTS],
                                            h1_t[c % 2][:, t * 128:(t + 1) * 128], routers[:, :],
                                            start=True, stop=True)
                last.then_inc(F("logits_done"), 1)

            def up(c, q):
                pe.wait_ge(F("h1t_ready"), c + 1)
                for b in range(2):
                    last = nc.tensor.matmul(bk[f"up{q}"][:, :], w1s[:, b, q, :], h1_t[c % 2][:, :],
                                            start=(b == 0), stop=(b == 1))
                last.then_inc(F(f"up{q}_done"), 1)

            def transpose_weights(c):
                pe.wait_ge(F("csplit_ready"), c + 1)
                for t in range(TILES):
                    last = nc.tensor.transpose(bk["combt"][0:PARTS, t * 64:(t + 1) * 64].bitcast(bf16),
                                               csplit[:, t, :, :, :].rearrange("p r s e -> p (r s e)"), ident16[:, :])
                last.then_inc(F("combt_done"), 1)

            def spread(c, q):
                pe.wait_ge(F("combt_ready"), c + 1)
                nc.tensor.matmul(bk[f"gate{q}"][:, :], select16[:, q, :], comb_t[:, :],
                                 start=True, stop=True).then_inc(F(f"gate{q}_done"), 1)

            def by_parity(ap):
                v = ap.rearrange("p (u m k) -> p m u k", m=2, k=128)
                return [v[:, m, :, :] for m in range(2)]

            down_out = [bk["down"][m * C:(m + 1) * C, 0:CT // 2].rearrange("p (u k) -> p u k", k=128) for m in range(2)]

            def down_residual(c):
                for m in range(2):
                    nc.tensor.matmul(bk["down"][:, 0:CT // 2].rearrange("p (u k) -> p u k", k=128), twice_c[:, m, :],
                                     by_parity(h1_t[c % 2][:, :])[m], start=(m == 0), stop=False)
                pe.wait_ge(F("combt_ready"), c + 1)
                for m in range(2):
                    last = nc.tensor.matmul(down_out[m], b2stack[:, :], by_parity(comb_t[:, :])[m],
                                            start=False, stop=False)
                last.then_inc(F("biases_done"), 1)

            def down(c, q):
                pe.wait_ge(F(f"hids{q}_ready"), c + 1)
                for m in range(2):
                    last = nc.tensor.matmul(down_out[m], w2c[:, q, :], by_parity(hids[:, q, :])[m],
                                            start=False, stop=(q == PAIRS - 1))
                last.then_inc(F(f"down{q}_done"), 1)

            def back_to_tokens(c):
                pe.wait_ge(F("y2t_ready"), c + 1)
                for u in range(2):
                    last = nc.tensor.transpose(bk["y2"][:, u * 128:(u + 1) * 128], y2t[:, u * 128:(u + 1) * 128],
                                               P("ident"))
                last.then_inc(F("back_done"), 1)

            for s in range(STEPS):
                if s < CHUNKS:
                    pe.wait_ge(F("rows_ready"), held(s - 1))
                if s > 0:
                    on(s, row_products, 0)
                if 0 <= s - 7 < CHUNKS:
                    pe.wait_ge(F("hids3_ready"), held(s - 8))
                if 7 <= s < 9:
                    pe.wait_ge(F("expand_ready"), held(s - 1))
                on(s - 7, spread, 1)
                if 0 <= s - 5 < CHUNKS:
                    pe.wait_ge(F("ht_ready"), held(s - 2))
                if 10 <= s < 13:
                    pe.wait_ge(F("logits_ready"), held(s - 6))
                on(s - 5, transpose_h1)
                if s > 0:
                    on(s, row_products, 1)
                if 0 <= s - 7 < CHUNKS:
                    pe.wait_ge(F("y2t_ready"), held(s - 8))
                on(s - 7, down_residual)
                if 0 <= s - 7 < CHUNKS:
                    pe.wait_ge(F("hid0_ready"), held(s - 7))
                on(s - 7, spread, 2)
                if 0 <= s - 8 < CHUNKS:
                    pe.wait_ge(F("ot_ready"), held(s - 9))
                if s == 8:
                    pe.wait_ge(F("rows_ready"), held(s - 1))
                on(s - 8, back_to_tokens)
                if 0 <= s - 6 < CHUNKS:
                    pe.wait_ge(F("hid3_ready"), held(s - 7))
                if s == 6:
                    pe.wait_ge(F("yc_ready"), held(s - 4))
                on(s - 6, up, 1)
                if 0 <= s - 3 < CHUNKS:
                    pe.wait_ge(F("hids0_ready"), held(s - 7))
                if 4 <= s < 7:
                    pe.wait_ge(F("gm_ready"), held(s - 4))
                on(s - 3, gram)
                if 0 <= s - 5 < CHUNKS:
                    pe.wait_ge(F("h1t_ready"), held(s - 5))
                on(s - 5, router)
                on(s - 7, down, 0)
                if s < CHUNKS:
                    pe.wait_ge(F("cols_ready"), held(s - 1))
                if s == 7:
                    pe.wait_ge(F("hids2_ready"), held(s - 7))
                on(s, transpose_rows)
                if s == 0:
                    keep_clock()
                if 0 <= s - 6 < CHUNKS:
                    pe.wait_ge(F("gm_ready"), held(s - 3))
                if 11 <= s < 14:
                    pe.wait_ge(F("hids0_ready"), held(s - 7))
                on(s - 6, up, 2)
                if 0 <= s - 1 < CHUNKS:
                    pe.wait_ge(F("logits_ready"), held(s - 5))
                if 2 <= s < 5:
                    pe.wait_ge(F("ht_ready"), held(s - 2))
                on(s - 1, tokens)
                if s == 1:
                    keep_clock()
                if 0 <= s - 7 < CHUNKS:
                    pe.wait_ge(F("hids1_ready"), held(s - 7))
                on(s - 7, spread, 3)
                if 0 <= s - 6 < CHUNKS:
                    pe.wait_ge(F("hids2_ready"), held(s - 7))
                if 6 <= s < 8:
                    pe.wait_ge(F("cols_ready"), held(s))
                on(s - 6, up, 0)
                if 0 <= s - 3 < CHUNKS:
                    pe.wait_ge(F("hid1_ready"), held(s - 6))
                if 4 <= s < 6:
                    pe.wait_ge(F("yc_ready"), held(s - 4))
                on(s - 3, attention)
                on(s - 7, down, 1)
                if 0 <= s - 6 < CHUNKS:
                    pe.wait_ge(F("hid2_ready"), held(s - 6))
                on(s - 6, transpose_weights)
                if s < CHUNKS:
                    pe.wait_ge(F("expand_ready"), held(s - 1))
                if s == 7:
                    pe.wait_ge(F("hids3_ready"), held(s - 7))
                on(s, column_products)
                if s == 0:
                    keep_clock()
                if 0 <= s - 1 < CHUNKS:
                    pe.wait_ge(F("n_ready"), held(s - 2))
                on(s - 1, head_centred)
                on(s - 7, down, 2)
                on(s - 7, down, 3)
                if 0 <= s - 6 < CHUNKS:
                    pe.wait_ge(F("combt_ready"), held(s - 6))
                on(s - 6, spread, 0)
                if 0 <= s - 6 < CHUNKS:
                    pe.wait_ge(F("yc_ready"), held(s - 3))
                if 11 <= s < 14:
                    pe.wait_ge(F("hid1_ready"), held(s - 6))
                on(s - 6, up, 3)


def resize_operator(size):
    scale = size / GRID
    at = (np.arange(GRID) + 0.5) * scale - 0.5
    w = np.maximum(0.0, 1.0 - np.abs(at[:, None] - np.arange(size)[None, :]) / scale)
    return w / w.sum(axis=1, keepdims=True)


def axis_operator():
    def haar(size, sign):
        m = np.zeros((size // 2, size))
        m[np.arange(size // 2), np.arange(0, size, 2)] = 0.5 ** 0.5
        m[np.arange(size // 2), np.arange(1, size, 2)] = sign * 0.5 ** 0.5
        return m
    low1, high1 = haar(SIDE, 1), haar(SIDE, -1)
    low2, high2 = haar(SIDE // 2, 1) @ low1, haar(SIDE // 2, -1) @ low1
    r1, r2 = resize_operator(SIDE // 2), resize_operator(SIDE // 4)
    return np.concatenate([r1 @ low1, r1 @ high1, r2 @ low2, r2 @ high2]).astype(np.float32)


def kernel(x, L0_tok_W, L0_tok_b, L0_attn_kln_weight, L0_attn_kln_bias, L0_attn_vln_weight, L0_attn_vln_bias,
           L0_ffn_router_w, L0_ffn_w1, L0_ffn_b1, L0_ffn_w2, L0_ffn_b2):
    import concourse.bacc as bacc
    from concourse.bass_utils import run_bass_kernel_spmd

    x = np.ascontiguousarray(x)
    blocks = [(FIRST_AT, np.zeros((128, FIRST), np.float32)), (SECOND_AT, np.zeros((128, SECOND), np.float32)),
              (MAIN_AT, np.zeros((128, MAIN), np.float32)),
              (PART_AT, np.zeros((PARTS, PART), np.float32))]

    def put(name, value):
        for at, block in blocks:
            if name in at:
                a, b = at[name]
                block[:, a:b] = np.asarray(value).reshape(block.shape[0], b - a)

    op = axis_operator()
    centre = np.eye(C) - 1 / C
    put("rows_op", op.T.reshape(128, 2, OPS))
    put("cols_op", op.T.reshape(2, 128, OPS).transpose(1, 0, 2))
    put("ident", np.eye(128))
    put("jmask", np.tile(np.eye(GRID), (128 // GRID, 1)))
    put("head_centre", np.tile(np.kron(np.eye(HEADS), np.eye(HEAD) - 1 / HEAD), (2, 1)))
    put("headmask", np.tile(np.kron(np.eye(HEADS), np.ones((HEAD, HEAD))) / TOKENS, (2, 1)))
    put("twice", np.tile(2 * np.eye(C), (2, 1)))
    put("twice_centre", np.tile(np.kron(np.eye(2).reshape(1, 4), 2 * centre), (2, 1)))
    sel = np.zeros((SPLIT, 4, EXPERTS, PAIRS, 2, FF), np.float32)
    for e in range(EXPERTS):
        sel[0, :SPLIT, e, e // 2, e % 2, :] = 0.5
    put("select", sel)
    i, j = np.arange(EXPERTS)[:, None], np.arange(EXPERTS)[None, :]
    put("before", np.broadcast_to(j < i, (128, EXPERTS, EXPERTS)))
    put("rank_limit", np.broadcast_to(np.arange(EXPERTS) - (EXPERTS - 1) + 1.5, (128, TILES, EXPERTS)))
    w = np.zeros((KINDS, KINDS, GRID, C), np.float32)
    for m, (a, b) in enumerate(MAPS):
        w[a, b] = np.broadcast_to(np.asarray(L0_tok_W)[m], (GRID, C))
    put("wtok", w)
    put("btok_col", np.tile(np.asarray(L0_tok_b), 2))
    for name, value in (("kw", L0_attn_kln_weight), ("kb", L0_attn_kln_bias), ("vw", L0_attn_vln_weight),
                        ("vb", L0_attn_vln_bias)):
        put(name, np.broadcast_to(np.asarray(value).reshape(C), (128, C)))
    put("w1", np.tile(np.asarray(L0_ffn_w1).transpose(1, 0, 2).reshape(C, EXPERTS * FF), (2, 1)))
    put("b1", np.asarray(L0_ffn_b1).reshape(PAIRS, 2 * FF).T)
    put("w2", np.asarray(L0_ffn_w2).reshape(PAIRS, 2 * FF, C).transpose(1, 0, 2))
    put("router", np.tile(np.asarray(L0_ffn_router_w).T, (2, 1)))
    put("b2", np.tile(np.asarray(L0_ffn_b2), (SPLIT * 4, 1)))

    nc = bacc.Bacc("TRN2", target_bir_lowering=False, num_devices=1)
    arrays = {"x_dram": x, "first_dram": blocks[0][1], "second_dram": blocks[1][1], "main_dram": blocks[2][1],
              "part_dram": blocks[3][1]}
    args = [nc.dram_tensor(name, a.shape, mybir.dt.float32, kind="ExternalInput").ap() for name, a in arrays.items()]
    out = nc.dram_tensor("out_dram", (IMAGES, TOKENS, C), mybir.dt.float32, kind="ExternalOutput").ap()
    vit_tower_kernel(nc, *args, out)
    r = run_bass_kernel_spmd(nc, [arrays], core_ids=[0])
    return r.results[0]["out_dram"]
```
